# Optimizing a Trainium2 kernel written in Bass

```python
import numpy as np
import jax
import jax.numpy as jnp

def _softmax(x, axis=-1):
    return jax.nn.softmax(x, axis=axis)
def _gelu(x):
    return jax.nn.gelu(x, approximate=True)
def _silu(x):
    return jax.nn.silu(x)
def _sigmoid(x):
    return jax.nn.sigmoid(x)
def _layernorm(x, axis=-1, eps=1e-5):
    m = jnp.mean(x, axis=axis, keepdims=True)
    v = jnp.var(x, axis=axis, keepdims=True)
    return (x - m) / jnp.sqrt(v + eps)
def _scatter_add(tgt, idx, src, axis=0):
    return tgt.at[idx].add(src)
def _segment_sum(src, seg, n):
    return jax.ops.segment_sum(src, seg, n)

kernel_name = 'mk_conv_preact_d2_conv_nhwc256_8068fd'

def setup_inputs(seed: int = 0):
    np.random.seed(seed)
    _w = jnp.asarray
    def _rec_inputs():
        import jax
        import jax.numpy as jnp
        _gk = jax.random.key(seed)
        x = -0.0005153 + 1.001 * jax.random.normal(jax.random.fold_in(_gk, 1), (4, 56, 56, 256), jnp.float32)
        return x
    x = _rec_inputs()
    def _L0_conv_setup():
        import jax, jax.numpy as jnp
        import numpy as np
        B, H, W, DIM = (4, 56, 56, 256)
        NUM_HEADS = 8
        HEAD_DIM = DIM // NUM_HEADS
        key = jax.random.key(seed)
        k1, k2, k3 = jax.random.split(key, 3)
        x = jax.random.normal(k1, (B, H, W, DIM), dtype=jnp.float32)
        w_qkv = jax.random.normal(k2, (DIM, 3 * NUM_HEADS * HEAD_DIM), dtype=jnp.float32) * 0.02
        w_proj = jax.random.normal(k3, (NUM_HEADS * HEAD_DIM, DIM), dtype=jnp.float32) * 0.02
        return {'x': x, 'w_qkv': w_qkv, 'w_proj': w_proj}
    _L0_conv_all = _L0_conv_setup()
    _L0_conv_in = {k: v for k, v in _L0_conv_all.items() if k in ('w_qkv', 'w_proj', )}
    del _L0_conv_all

    def _L1_conv_setup():
        import jax, jax.numpy as jnp
        import numpy as np
        key = jax.random.key(seed)
        ks = jax.random.split(key, 4)
        B, H, W, C = (4, 256, 256, 256)
        Ck = C // 8
        x = jax.random.normal(ks[0], (B, H, W, C), dtype=jnp.float32)
        Wf = jax.random.normal(ks[1], (C, Ck), dtype=jnp.float32) / np.sqrt(C)
        Wg = jax.random.normal(ks[2], (C, Ck), dtype=jnp.float32) / np.sqrt(C)
        Wh = jax.random.normal(ks[3], (C, C), dtype=jnp.float32) / np.sqrt(C)
        bf = jnp.zeros((Ck,), jnp.float32)
        bg = jnp.zeros((Ck,), jnp.float32)
        bh = jnp.zeros((C,), jnp.float32)
        return {'x': x, 'Wf': Wf, 'bf': bf, 'Wg': Wg, 'bg': bg, 'Wh': Wh, 'bh': bh}
    _L1_conv_all = _L1_conv_setup()
    _L1_conv_in = {k: v for k, v in _L1_conv_all.items() if k in ('Wf', 'bf', 'Wg', 'bg', 'Wh', 'bh', )}
    del _L1_conv_all

    return {
        "x": x,
        "L0_conv_w_qkv": _L0_conv_in["w_qkv"],
        "L0_conv_w_proj": _L0_conv_in["w_proj"],
        "L1_conv_Wf": _L1_conv_in["Wf"],
        "L1_conv_bf": _L1_conv_in["bf"],
        "L1_conv_Wg": _L1_conv_in["Wg"],
        "L1_conv_bg": _L1_conv_in["bg"],
        "L1_conv_Wh": _L1_conv_in["Wh"],
        "L1_conv_bh": _L1_conv_in["bh"],
    }

def reference(x, L0_conv_w_qkv, L0_conv_w_proj, L1_conv_Wf, L1_conv_bf, L1_conv_Wg, L1_conv_bg, L1_conv_Wh, L1_conv_bh):
    import jax
    import jax.numpy as jnp
    def _L0_conv_ref(x, w_qkv, w_proj):
        import jax, jax.numpy as jnp
        import numpy as np
        B, H, W, DIM = (4, 56, 56, 256)
        NUM_HEADS = 8
        HEAD_DIM = DIM // NUM_HEADS
        b, h, w, c = x.shape
        nh, hd = (NUM_HEADS, HEAD_DIM)
        scale = hd ** (-0.25)
        qkv = jnp.einsum('bhwc,cd->bhwd', x, w_qkv)
        qkv = qkv.reshape(b, h * w, 3, nh, hd).transpose(2, 0, 3, 1, 4)
        q, k, v = (qkv[0], qkv[1], qkv[2])
        attn = jnp.einsum('bnqd,bnkd->bnqk', q * scale, k * scale)
        attn = jax.nn.softmax(attn, axis=-1)
        out = jnp.einsum('bnqk,bnkd->bnqd', attn, v)
        out = out.transpose(0, 2, 1, 3).reshape(b, h, w, nh * hd)
        return jnp.einsum('bhwc,cd->bhwd', out, w_proj)

    def _L1_conv_ref(x, Wf, bf, Wg, bg, Wh, bh):
        import jax, jax.numpy as jnp
        import numpy as np
        f = jnp.einsum('bhwc,ck->bhwk', x, Wf) + bf
        g = jnp.einsum('bhwc,ck->bhwk', x, Wg) + bg
        h = jnp.einsum('bhwc,co->bhwo', x, Wh) + bh
        scores = jnp.einsum('bhik,bhjk->bhij', f, g)
        attn = jax.nn.sigmoid(scores)
        out = jnp.einsum('bhij,bhjo->bhio', attn, h)
        return out

    def _gn(v, G=32, eps=1e-5):
        B_, H_, W_, C_ = v.shape
        g = v.reshape(B_, H_, W_, G, C_ // G)
        m = jnp.mean(g, axis=(1, 2, 4), keepdims=True)
        s = jnp.var(g, axis=(1, 2, 4), keepdims=True)
        return ((g - m) / jnp.sqrt(s + eps)).reshape(v.shape)

    def _ln_c(v, eps=1e-6):
        m = jnp.mean(v, axis=-1, keepdims=True)
        s = jnp.var(v, axis=-1, keepdims=True)
        return (v - m) / jnp.sqrt(s + eps)

    def _ln_t(v, eps=1e-5):
        m = jnp.mean(v, axis=-1, keepdims=True)
        s = jnp.var(v, axis=-1, keepdims=True)
        return (v - m) / jnp.sqrt(s + eps)

    def _to_tokens(v):
        B_, H_, W_, C_ = v.shape
        return v.reshape(B_, H_ * W_, C_)
    def _from_tokens(t, like):
        return t.reshape(like.shape)

    x = x + _L0_conv_ref(_gn(x), L0_conv_w_qkv, L0_conv_w_proj)
    x = x + _L1_conv_ref(_gn(x), L1_conv_Wf, L1_conv_bf, L1_conv_Wg, L1_conv_bg, L1_conv_Wh, L1_conv_bh)
    return x


_drawn_inputs = setup_inputs


def setup_inputs(seed=0):
    import zlib

    import numpy as np

    out = dict(_drawn_inputs(seed))
    spreads = {'L1_conv_bf': (0.0, 0.1), 'L1_conv_bg': (0.0, 0.1), 'L1_conv_bh': (0.0, 0.1)}
    factors = {'L0_conv_w_qkv': 7.181, 'L0_conv_w_proj': 7.202}
    for name, (base, spread) in spreads.items():
        noise = np.random.default_rng([zlib.crc32(name.encode()), seed]).standard_normal(out[name].shape)
        drawn = base * np.exp(spread * noise) if base else spread * noise
        out[name] = jnp.asarray(drawn.astype(out[name].dtype))
    for name, factor in factors.items():
        out[name] = (out[name] * factor).astype(out[name].dtype)
    return out
```

```python
from contextlib import ExitStack

import concourse.bass as bass
from concourse import mybir

F32 = mybir.dt.float32
F32R = mybir.dt.float32r
BF16 = mybir.dt.bfloat16
I32 = mybir.dt.int32
ACT = mybir.ActivationFunctionType
ALU = mybir.AluOpType
AX = mybir.AxisListType

P = 128
C = 256
CH = C // P
SIDE = 56
T = SIDE * SIDE
HD = 32
HG = 4
G = 2
CW = 448
NC = T // CW
TW = 2 * SIDE
TPC = CW // TW
NT = T // TW
NK = (T + P - 1) // P
KLAST = T - (NK - 1) * P
GSIZE = C // 32
EPS = 1e-5
SCALE = float(HD) ** -0.25

SHIFT = 40.0
SCORE_BOUND = 100.0
MEAN_BOUND = 10.0
WV_BOUND = 1e3
SLACK = 1.02


def keys(kt):
    return KLAST if kt == NK - 1 else P


def build_consts(nc, ctx):
    def sb(name, shape, dt=F32):
        return ctx.enter_context(nc.sbuf_tensor(name, shape, dt))

    k = dict(
        ident=sb("ident", [P, P]),
        group_avg=sb("group_avg", [P, P]),
        head_sum=sb("head_sum", [P, P]),
        head_sum_bf=sb("head_sum_bf", [P, P], BF16),
        ones=sb("ones", [P, HD]),
        minus_half=sb("minus_half", [P, CH]),
        row_mask=sb("row_mask", [TW, TW]),
        norm_max=sb("norm_max", [P, 4, 4]),
        xn_mean=sb("xn_mean", [P, CH, 4]),
        bounded=sb("bounded", [P, 1], I32),
    )
    made = ctx.enter_context(nc.semaphore("consts_made"))
    count = [0]
    with nc.Block() as block:
        @block.gpsimd
        def _(pool):
            def step(ins):
                ins.then_inc(made, 1)
                count[0] += 1
                pool.wait_ge(made, count[0])

            def blocks(t, value, width):
                n = t.shape[1] // width
                v = t[:].rearrange("p (n w) -> p n w", w=width)
                step(nc.gpsimd.memset(t[:], value))
                step(nc.gpsimd.affine_select(out=v, in_=v, compare_op=ALU.is_ge, fill=0.0, base=0,
                                             pattern=[[-width, n], [0, width]], channel_multiplier=1))
                step(nc.gpsimd.affine_select(out=v, in_=v, compare_op=ALU.is_ge, fill=0.0, base=width - 1,
                                             pattern=[[width, n], [0, width]], channel_multiplier=-1))

            step(nc.gpsimd.memset(k["ident"][:], 0.0))
            step(nc.gpsimd.affine_select(out=k["ident"][:], in_=k["ident"][:], compare_op=ALU.not_equal, fill=1.0,
                                         base=0, pattern=[[-1, P]], channel_multiplier=1))
            blocks(k["group_avg"], 1.0 / GSIZE, GSIZE)
            blocks(k["head_sum"], 1.0, HD)
            blocks(k["row_mask"], 1.0, SIDE)
            step(nc.gpsimd.tensor_copy(k["head_sum_bf"][:], k["head_sum"][:]))
            step(nc.gpsimd.memset(k["ones"][:], 1.0))
            step(nc.gpsimd.memset(k["minus_half"][:], -0.5))
    return k


START = 1


class Turn:

    def __init__(self, eng, value, offset=0, kept=None):
        self.eng, self.value, self.offset = eng, value, offset
        self.kept = {} if kept is None else kept

    def __mul__(self, n):
        if isinstance(self.value, int):
            return (self.value + self.offset) * n
        if n not in self.kept:
            self.kept[n] = self.eng.snap(self.value * n)
        return self.kept[n] + self.offset * n

    __rmul__ = __mul__

    def __add__(self, n):
        return Turn(self.eng, self.value, self.offset + n, self.kept)


def at(turn):
    return turn.value + turn.offset if isinstance(turn, Turn) else turn


class GroupNorm:

    def __init__(self, nc, sb, sem, k, psum):
        self.nc, self.k, self.psum = nc, k, psum
        self.chunk_stats = sb("chunk_stats", [P, CH, NC, 6])
        self.moments = sb("moments", [P, CH, 2])
        self.off = sb("off", [P, CH])
        self.spread_t = sb("spread", [P, CH])
        self.mean = sb("mean", [P, CH])
        self.var = sb("var", [P, CH])
        self.rstd_t = sb("rstd", [P, CH])
        self.stat_done = sem("stat_done")
        self.aggregated = sem("aggregated")
        self.means_avg = sem("means_avg")
        self.spread_done = sem("spread_done")
        self.spread_avg = sem("spread_avg")
        self.var_done = sem("var_done")
        self.rstd_done = sem("rstd_done")
        self.gate = sem("gate")

    def stats(self, src, c, ch):
        self.nc.vector.bn_stats(self.chunk_stats[:, ch, c, :],
                                src[:, ch, c * CW:(c + 1) * CW]).then_inc(self.stat_done, 1)

    def aggregate(self, dve, b):
        dve.wait_ge(self.stat_done, START + CH * NC * (b + 1))
        dve.sem_inc(self.gate, 1)
        for ch in range(CH):
            self.nc.vector.bn_aggr(self.moments[:, ch, :], self.chunk_stats[:, ch, :, :]) \
                .then_inc(self.aggregated, 1)

    def average_means(self, pe, b):
        pe.wait_ge(self.aggregated, START + CH * (b + 1))
        self.nc.tensor.matmul(self.psum[:, 0:CH], self.k["group_avg"][:], self.moments[:, :, 0],
                              start=True, stop=True).then_inc(self.means_avg, 1)

    def spread(self, dve, b):
        v = self.nc.vector
        dve.wait_ge(self.means_avg, START + 1 * (b + 1))
        v.tensor_copy(self.mean[:], self.psum[:, 0:CH]).then_inc(self.spread_done, 1)
        dve.wait_ge(self.spread_done, START + 3 * b + 1)
        v.tensor_tensor(self.off[:], self.moments[:, :, 0], self.mean[:], ALU.subtract) \
            .then_inc(self.spread_done, 1)
        dve.wait_ge(self.spread_done, START + 3 * b + 2)
        v.tensor_tensor(self.spread_t[:], self.off[:], self.off[:], ALU.mult).then_inc(self.spread_done, 1)
        dve.wait_ge(self.spread_done, START + 3 * b + 3)
        v.tensor_tensor(self.var[:], self.spread_t[:], self.moments[:, :, 1], ALU.add) \
            .then_inc(self.var_done, 1)

    def average_spread(self, pe, b):
        pe.wait_ge(self.var_done, START + 2 * b + 1)
        self.nc.tensor.matmul(self.psum[:, CH:2 * CH], self.k["group_avg"][:], self.var[:],
                              start=True, stop=True).then_inc(self.spread_avg, 1)

    def variance(self, dve, b):
        dve.wait_ge(self.spread_avg, START + 1 * (b + 1))
        self.nc.vector.tensor_scalar(self.spread_t[:], self.psum[:, CH:2 * CH], EPS, None, ALU.add) \
            .then_inc(self.var_done, 1)

    def rstd(self, pool, b):
        pool.wait_ge(self.var_done, START + 2 * b + 2)
        self.nc.gpsimd.tensor_tensor(self.rstd_t[:], self.spread_t[:], self.k["minus_half"][:], ALU.pow) \
            .then_inc(self.rstd_done, 1)

    def norm(self, dst, src, c, ch):
        s = slice(c * CW, (c + 1) * CW)
        return self.nc.vector.tensor_scalar(dst[:, ch, s], src[:, ch, s], self.mean[:, ch:ch + 1],
                                            self.rstd_t[:, ch:ch + 1], ALU.subtract, ALU.mult)


def part_a(nc, k, B, x, w_qkv, d):
    NQ = 4 * NC
    with ExitStack() as ctx:
        def sb(name, shape, dt=F32):
            return ctx.enter_context(nc.sbuf_tensor("a_" + name, shape, dt))

        sems = []

        def sem(name):
            sems.append(ctx.enter_context(nc.semaphore("a_" + name)))
            return sems[-1]

        bank = [ctx.enter_context(nc.psum_tensor(f"a_bank{i}", [P, 512], F32)) for i in range(8)]
        bank_t, bank_q, bank_n, bank_v = bank[0:2], bank[2:5], bank[5], bank[6:8]
        x_in = sb("x_in", [TW, NT, C])
        xT = sb("xT", [P, CH, T])
        xn = sb("xn", [P, CH, T])
        w = sb("w", [P, CH, 3 * C])
        parts = sb("parts", [P, 4, 2, CW], F32R)
        square = sb("square", [P, 3, CW], BF16)
        v_st = sb("v_st", [P, G, NK, HG * HD])
        item_max = sb("item_max", [P, NQ])
        kmean2 = sb("kmean2", [P, G * B])
        bound = sb("bound", [P, 2 * G * B + 1])
        worst = sb("worst", [P, 2])

        w_loaded, x_stored, v_stored = sem("w_loaded"), sem("x_stored"), sem("v_stored")
        x_loaded = [sem(f"x_loaded{c}") for c in range(NC)]
        part_stored = [sem(f"part_stored{j}") for j in range(4)]
        t_done, t_act, t_dve = sem("t_done"), sem("t_act"), sem("t_dve")
        normed = sem("normed")
        q_done, q_high, q_low = sem("q_done"), sem("q_high"), sem("q_low")
        squared, summed, max_taken = sem("squared"), sem("summed"), sem("max_taken")
        v_done, v_act, v_dve, v_zero = sem("v_done"), sem("v_act"), sem("v_dve"), sem("v_zero")
        end_pe, end_dve, end_pool, image_max = sem("end_pe"), sem("end_dve"), sem("end_pool"), sem("image_max")
        mean_saved = sem("mean_saved")
        gn = GroupNorm(nc, sb, sem, k, bank_n)
        x_tok = x.rearrange("b h w c -> b (h w) c").rearrange("b (t p) c -> b p t c", p=TW)
        VA, VD = (NK + 1) // 2, NK // 2

        with nc.Block() as block:
            @block.sync
            def _(sp):
                for s in sems:
                    sp.sem_inc(s, START)

                def load_x(b, c):
                    sp.dma_start(x_in[:, c * TPC:(c + 1) * TPC, :], x_tok[at(b), :, c * TPC:(c + 1) * TPC, :]) \
                        .then_inc(x_loaded[c], 16)

                def image(b, more):
                    sp.wait_ge(t_act, START + NC * (b + 1))
                    sp.wait_ge(t_dve, START + NC * (b + 1))
                    sp.dma_start(d["xT"][at(b)].rearrange("h p t -> p h t"), xT[:]).then_inc(x_stored, 16)
                    if more:
                        for c in range(NC):
                            load_x(b + 1, c)
                    for c in range(NC):
                        for j in range(4):
                            dst = d["q" if j < 2 else "k"][at(b), j % 2]
                            sp.wait_ge(q_low, START + NQ * b + 4 * c + j + 1)
                            sp.dma_start(dst[:, :, c * CW:(c + 1) * CW].rearrange("s p t -> p s t"),
                                         parts[:, j].bitcast(F32)).then_inc(part_stored[j], 16)
                    sp.wait_ge(v_act, START + VA * (b + 1))
                    sp.wait_ge(v_dve, START + VD * (b + 1))
                    sp.dma_start(d["v"][at(b)].rearrange("g p k n -> p g k n"), v_st[:]).then_inc(v_stored, 16)

                for c in range(NC):
                    load_x(0, c)
                    if c == 0:
                        sp.dma_start(w[:], w_qkv.rearrange("(h p) n -> p h n", p=P)).then_inc(w_loaded, 16)
                with sp.Fori(0, B - 1) as i:
                    b = Turn(sp, i)
                    image(b, True)
                image(B - 1, False)
                sp.wait_ge(x_stored, START + 16 * B)
                sp.wait_ge(v_stored, START + 16 * B)
                for j in range(4):
                    sp.wait_ge(part_stored[j], START + 16 * NC * B)

            @block.tensor
            def _(pe):
                def transposes(b):
                    for c in range(NC):
                        pe.wait_ge(x_loaded[c], START + 16 * (b + 1))
                        for ch, freed in ((0, t_act), (1, t_dve)):
                            if not (isinstance(b, int) and b == 0 and c == 0):
                                pe.wait_ge(freed, START + NC * b + c)
                            for t in range(TPC):
                                last = nc.tensor.transpose(bank_t[ch][:, t * TW:(t + 1) * TW],
                                                           x_in[:, c * TPC + t, ch * P:(ch + 1) * P],
                                                           k["ident"][0:TW, 0:TW])
                            last.then_inc(t_done, 1)

                def head_norms(b, i):
                    pe.wait_ge(squared, START + NQ * b + i + 1)
                    pe.wait_ge(max_taken, START + NQ * b + i)
                    nc.tensor.matmul(bank_n[:, 0:CW], k["head_sum_bf"][:], square[:, i % 3, :],
                                     start=True, stop=True).then_inc(summed, 1)

                def q_and_k(b):
                    for i in range(NQ):
                        c, j = divmod(i, 4)
                        if j == 0:
                            pe.wait_ge(normed, START + CH * (NC * b + c + 1))
                        pe.wait_ge(q_low, START + NQ * b + max(0, i - 2))
                        for ch in range(CH):
                            last = nc.tensor.matmul(bank_q[i % 3][:, 0:CW], w[:, ch, j * P:(j + 1) * P],
                                                    xn[:, ch, c * CW:(c + 1) * CW],
                                                    start=ch == 0, stop=ch == CH - 1)
                        last.then_inc(q_done, 1)
                        if i >= 2:
                            head_norms(b, i - 2)
                    for i in range(NQ - 2, NQ):
                        head_norms(b, i)

                def values(b, more):
                    for kt in range(NK):
                        freed, n = (v_dve, VD) if kt % 2 else (v_act, VA)
                        pe.wait_ge(freed, START + n * b + kt // 2)
                        m = keys(kt)
                        for ch in range(CH):
                            last = nc.tensor.matmul(bank_v[kt % 2][0:m, 0:C], xn[:, ch, kt * P:kt * P + m],
                                                    w[:, ch, 2 * C:3 * C], start=ch == 0, stop=ch == CH - 1)
                        last.then_inc(v_done, 1)
                        if more and kt == 10:
                            pe.wait_ge(max_taken, START + NQ * (b + 1))
                            gn.average_means(pe, b + 1)
                        if more and kt == 17:
                            gn.average_spread(pe, b + 1)

                pe.wait_ge(w_loaded, START + 16)
                transposes(0)
                gn.average_means(pe, 0)
                gn.average_spread(pe, 0)
                with pe.Fori(0, B - 1) as i:
                    b = Turn(pe, i)
                    q_and_k(b)
                    transposes(b + 1)
                    values(b, True)
                q_and_k(B - 1)
                values(B - 1, False)
                pe.wait_ge(mean_saved, START + B)
                pe.wait_ge(max_taken, START + NQ * B)
                for g in range(G):
                    for ch in range(CH):
                        last = nc.tensor.matmul(bank_n[:, g * B:(g + 1) * B],
                                                w[:, ch, C + g * P:C + (g + 1) * P], k["xn_mean"][:, ch, 0:B],
                                                start=ch == 0, stop=ch == CH - 1)
                last.then_inc(end_pe, 1)
                pe.wait_ge(end_dve, START + 2)
                nc.tensor.matmul(bank_q[0][:, 0:G * B], k["head_sum"][:], kmean2[:], start=True, stop=True) \
                    .then_inc(end_pe, 1)

            @block.scalar
            def _(act):
                def evacuate_x(b):
                    for c in range(NC):
                        if c == 0 and not isinstance(b, int):
                            act.wait_ge(normed, START + CH * NC * b)
                            act.wait_ge(x_stored, START + 16 * b)
                        act.wait_ge(t_done, START + CH * (NC * b + c) + 1)
                        nc.scalar.copy(xT[:, 0, c * CW:(c + 1) * CW], bank_t[0][:, 0:CW]).then_inc(t_act, 1)

                def high_parts(b):
                    for i in range(NQ):
                        c, j = divmod(i, 4)
                        act.wait_ge(q_done, START + NQ * b + i + 1)
                        act.wait_ge(part_stored[j], START + 16 * (NC * b + c))
                        if i >= 4:
                            act.wait_ge(squared, START + NQ * b + i - 3)
                        nc.scalar.activation(parts[:, j, 0, :], bank_q[i % 3][:, 0:CW], ACT.Copy, scale=SCALE) \
                            .then_inc(q_high, 1)

                def evacuate_v(b):
                    act.wait_ge(v_stored, START + 16 * b)
                    for kt in range(0, NK, 2):
                        m = keys(kt)
                        act.wait_ge(v_done, START + NK * b + kt + 1)
                        nc.scalar.copy(v_st[0:m, :, kt, :], bank_v[0][0:m, 0:C].rearrange("p (g n) -> p g n", g=G)) \
                            .then_inc(v_act, 1)

                evacuate_x(0)
                act.wait_ge(v_zero, START + 1)
                with act.Fori(0, B - 1) as i:
                    b = Turn(act, i)
                    high_parts(b)
                    evacuate_x(b + 1)
                    evacuate_v(b)
                high_parts(B - 1)
                evacuate_v(B - 1)

            @block.gpsimd
            def _(pool):
                def squares(b):
                    for i in range(NQ):
                        pool.wait_ge(q_high, START + NQ * b + i + 1)
                        pool.wait_ge(summed, START + NQ * b + max(0, i - 2))
                        high = parts[:, i % 4, 0, :].bitcast(F32)
                        nc.gpsimd.tensor_tensor(square[:, i % 3, :], high, high, ALU.mult).then_inc(squared, 1)

                nc.gpsimd.memset(v_st[KLAST:P, :, NK - 1, :], 0.0).then_inc(v_zero, 1)
                pool.wait_ge(v_zero, START + 1)
                gn.rstd(pool, 0)
                with pool.Fori(0, B - 1) as i:
                    b = Turn(pool, i)
                    squares(b)
                    pool.wait_ge(normed, START + CH * NC * (b + 1))
                    gn.rstd(pool, b + 1)
                squares(B - 1)
                pool.wait_ge(end_dve, START + 3 + 4)
                nc.gpsimd.partition_all_reduce(worst[:, 1:2], worst[:, 0:1], P, bass.bass_isa.ReduceOp.max) \
                    .then_inc(end_pool, 1)

            @block.vector
            def _(dve):
                v = nc.vector

                def evacuate_x(b):
                    for c in range(NC):
                        if c == 0 and not isinstance(b, int):
                            dve.wait_ge(normed, START + CH * NC * b)
                            dve.wait_ge(x_stored, START + 16 * b)
                        dve.wait_ge(t_done, START + CH * (NC * b + c + 1))
                        v.tensor_copy(xT[:, 1, c * CW:(c + 1) * CW], bank_t[1][:, 0:CW]).then_inc(t_dve, 1)
                        dve.wait_ge(t_act, START + NC * b + c + 1)
                        gn.stats(xT, c, 0)
                        dve.wait_ge(t_dve, START + NC * b + c + 1)
                        gn.stats(xT, c, 1)

                def norm(b):
                    dve.wait_ge(gn.rstd_done, START + 1 * (b + 1))
                    v.tensor_tensor(k["xn_mean"][:, :, at(b)], gn.off[:], gn.rstd_t[:], ALU.mult) \
                        .then_inc(mean_saved, 1)
                    dve.wait_ge(v_done, START + NK * b)
                    for c in range(NC):
                        for ch in range(CH):
                            gn.norm(xn, xT, c, ch).then_inc(normed, 1)

                def take_max(b, i):
                    dve.wait_ge(summed, START + NQ * b + i + 1)
                    v.reduce_max(item_max[:, i:i + 1], bank_n[:, 0:CW], AX.X).then_inc(max_taken, 1)

                def low_parts(b):
                    for i in range(NQ):
                        j = i % 4
                        dve.wait_ge(q_high, START + NQ * b + i + 1)
                        v.scalar_tensor_tensor(out=parts[:, j, 1, :], in0=bank_q[i % 3][:, 0:CW], scalar=SCALE,
                                               in1=parts[:, j, 0, :].bitcast(F32), op0=ALU.mult,
                                               op1=ALU.subtract).then_inc(q_low, 1)
                        if i >= 3:
                            take_max(b, i - 3)
                    for i in range(NQ - 3, NQ):
                        take_max(b, i)
                    dve.wait_ge(max_taken, START + NQ * (b + 1))
                    v.tensor_reduce(k["norm_max"][:, at(b), :], item_max[:].rearrange("p (c j) -> p j c", j=4),
                                    AX.X, ALU.max).then_inc(image_max, 1)

                def values(b, more):
                    dve.wait_ge(v_stored, START + 16 * b)
                    if more:
                        gn.aggregate(dve, b + 1)
                    for kt in range(1, NK, 2):
                        dve.wait_ge(v_done, START + NK * b + kt + 1)
                        v.tensor_copy(v_st[:, :, kt, :], bank_v[1][:, 0:C].rearrange("p (g n) -> p g n", g=G)) \
                            .then_inc(v_dve, 1)
                        if more and kt == 13:
                            gn.spread(dve, b + 1)
                        if more and kt == 21:
                            gn.variance(dve, b + 1)

                evacuate_x(0)
                gn.aggregate(dve, 0)
                gn.spread(dve, 0)
                gn.variance(dve, 0)
                with dve.Fori(0, B - 1) as i:
                    b = Turn(dve, i)
                    norm(b)
                    low_parts(b)
                    dve.wait_ge(image_max, START + 1 * (b + 1))
                    evacuate_x(b + 1)
                    values(b, True)
                norm(B - 1)
                low_parts(B - 1)
                values(B - 1, False)

                n = G * B
                dve.wait_ge(end_pe, START + 1)
                v.tensor_scalar(kmean2[:], bank_n[:, 0:n], SCALE, None, ALU.mult).then_inc(end_dve, 1)
                dve.wait_ge(end_dve, START + 1)
                v.tensor_tensor(kmean2[:], kmean2[:], kmean2[:], ALU.mult).then_inc(end_dve, 1)
                dve.wait_ge(image_max, START + B)
                q2 = k["norm_max"][:, 0:B, 0:G]
                k2 = k["norm_max"][:, 0:B, G:2 * G]
                v.scalar_tensor_tensor(out=bound[:, 0:n].rearrange("p (b g) -> p b g", g=G), in0=q2,
                                       scalar=(SLACK / SCORE_BOUND) ** 2, in1=k2, op0=ALU.mult, op1=ALU.mult) \
                    .then_inc(end_dve, 1)
                dve.wait_ge(end_pe, START + 2)
                v.scalar_tensor_tensor(out=bound[:, n:2 * n].rearrange("p (b g) -> p b g", g=G), in0=q2,
                                       scalar=(SLACK / MEAN_BOUND) ** 2,
                                       in1=bank_q[0][:, 0:n].rearrange("p (g b) -> p b g", g=G),
                                       op0=ALU.mult, op1=ALU.mult).then_inc(end_dve, 1)
                v.tensor_reduce(worst[:, 0:1], w[:, :, 2 * C:3 * C], AX.XY, ALU.max, apply_absolute_value=True) \
                    .then_inc(end_dve, 1)
                dve.wait_ge(end_dve, START + 5)
                v.tensor_scalar(bound[:, 2 * n:2 * n + 1], worst[:, 0:1], 1.0 / WV_BOUND, None, ALU.mult) \
                    .then_inc(end_dve, 1)
                dve.wait_ge(end_dve, START + 6)
                v.reduce_max(worst[:, 0:1], bound[:, 0:2 * n + 1], AX.X).then_inc(end_dve, 1)
                dve.wait_ge(end_pool, START + 1)
                v.tensor_scalar(k["bounded"][:], worst[:, 1:2], 1.0, None, ALU.is_le).then_inc(end_dve, 1)


def part_b(nc, k, B, d):
    NP = 2 * NK
    U = G * NC
    SLOTS = 3
    RING = 5
    GRP = 5
    NG = NK // GRP
    ADDS = 2 * (GRP - 1) * NG
    with ExitStack() as ctx:
        def sb(name, shape, dt=F32):
            return ctx.enter_context(nc.sbuf_tensor("b_" + name, shape, dt))

        sems = []

        def sem(name):
            sems.append(ctx.enter_context(nc.semaphore("b_" + name)))
            return sems[-1]

        scores = ctx.enter_context(nc.psum_tensor("b_scores", [P, SLOTS, 2, 512], F32))
        out_ps = ctx.enter_context(nc.psum_tensor("b_out", [P, 512], F32))
        sum_ps = ctx.enter_context(nc.psum_tensor("b_sum", [P, 512], F32))
        k_st = [sb(f"k_st{g}", [P, HG, T], F32R) for g in range(G)]
        v_st = [sb(f"v_st{g}", [P, NK, HG * HD]) for g in range(G)]
        q_st = sb("q_st", [P, 2, HG, CW], F32R)
        prob = sb("prob", [P, RING, HG, CW])
        part = sb("part", [P, 2, HG, CW])
        out_sb = sb("out_sb", [P, CW])
        inv = sb("inv", [P, CW])
        res = sb("res", [P, 2, CW])
        run_max = prob[:, 0]
        all_max = sb("all_max", [P, HG, CW])

        k_loaded = [sem(f"k_loaded{g}") for g in range(G)]
        v_loaded = [sem(f"v_loaded{g}") for g in range(G)]
        q_loaded = [sem(f"q_loaded{s}") for s in range(2)]
        scored, exps, pv_done, added = sem("scored"), sem("exps"), sem("pv_done"), sem("added")
        summed, sum_read, out_copied, res_done = sem("summed"), sem("sum_read"), sem("out_copied"), sem("res_done")
        res_stored = [sem(f"res_stored{s}") for s in range(2)]
        max_read, max_all, shifted, gate = sem("max_read"), sem("max_all"), sem("shifted"), sem("gate")

        def image_units(eng, b, unit):
            def one(g, l, i, ahead):
                u = Turn(eng, eng.snap(U * b + l + 2 * i))
                unit(g, u, l % 2, Turn(eng, eng.snap(U // 2 * b + l // 2 + i)), ahead)

            for g in range(G):
                with eng.Fori(0, NC // 2) as i:
                    for r in range(2):
                        one(g, g * NC + r, i, None)
                one(g, g * NC + NC - 1, 0, 1 - g)

        def branch(eng, fast, exact):
            ok = eng.value_load(k["bounded"][0:1, 0:1])
            with eng.If(ok > 0):
                fast()
            with eng.Else():
                exact()

        def loads(sp, pairs):
            def load_k(b, g):
                for rep in range(2):
                    for s in range(2):
                        row = 64 * rep + 32 * s
                        sp.dma_start(k_st[g][row:row + 32].bitcast(F32), d["k"][at(b), g, s].rearrange("(h e) t -> e h t", e=HD)) \
                            .then_inc(k_loaded[g], 16)
                sp.dma_start(v_st[g][:], d["v"][at(b), g]).then_inc(v_loaded[g], 16)

            def load_q(b, l):
                g, c = divmod(l, NC)
                for s in range(2):
                    for rep in range(2):
                        row = 64 * s + 32 * rep
                        sp.dma_start(q_st[row:row + 32, l % 2].bitcast(F32),
                                     d["q"][at(b), g, s, :, c * CW:(c + 1) * CW].rearrange("(h e) t -> e h t", e=HD)) \
                            .then_inc(q_loaded[l % 2], 16)

            def image(b, more):
                first = Turn(sp, U * b)
                sp.wait_ge(scored, START + pairs * first)
                sp.wait_ge(pv_done, START + NK * (first + 1))
                load_k(b, 1)
                for l in range(U):
                    u = first + l
                    sp.wait_ge(scored, START + pairs * u)
                    if l + 1 < U:
                        load_q(b, l + 1)
                    elif more:
                        load_q(b + 1, 0)
                    else:
                        sp.sem_inc(q_loaded[0], 64)
                    if l == NC:
                        sp.wait_ge(pv_done, START + NK * (u + 1))
                        if more:
                            load_k(b + 1, 0)
                        else:
                            sp.sem_inc(k_loaded[0], 64)
                    g, c = divmod(l, NC)
                    sp.wait_ge(res_done, START + 1 * (u + 1))
                    sp.dma_start(d["att"][at(b), g, :, c * CW:(c + 1) * CW], res[:, l % 2, :]) \
                        .then_inc(res_stored[l % 2], 16)

            load_q(0, 0)
            load_k(0, 0)
            with sp.Fori(0, B - 1) as i:
                b = Turn(sp, i)
                image(b, True)
            image(B - 1, False)
            for s in range(2):
                sp.wait_ge(res_stored[s], START + 16 * (U // 2) * B)

        def score_pair(g, slot, p):
            kt, hp = divmod(p, 2)
            m = keys(kt)
            for e in range(2):
                h = 2 * hp + e
                last = nc.tensor.matmul(scores[0:m, p % SLOTS, e, 0:CW], k_st[g][:, h, kt * P:kt * P + m],
                                        q_st[:, slot, h, :], start=True, stop=True)
            last.then_inc(scored, 1)

        def weighted_values(pe, u, g, kt):
            pe.wait_ge(exps, START + NP * (u + 1) + 2 * kt + 2)
            if kt == 0:
                pe.wait_ge(out_copied, START + 1 * u)
            for h in range(HG):
                last = nc.tensor.matmul(out_ps[h * HD:(h + 1) * HD, 0:CW], v_st[g][:, kt, h * HD:(h + 1) * HD],
                                        prob[:, kt % RING, h, :], start=kt == 0, stop=kt == NK - 1)
            last.then_inc(pv_done, 1)

        def row_sums(pe, u, j):
            pe.wait_ge(added, START + ADDS * (u + 1) + (ADDS // NG) * (j + 1))
            if j == 0:
                pe.wait_ge(sum_read, START + 1 * u)
            for h in range(HG):
                last = nc.tensor.matmul(sum_ps[h * HD:(h + 1) * HD, 0:CW], k["ones"][:], part[:, j % 2, h, :],
                                        start=j == 0, stop=j == NG - 1)
            last.then_inc(summed, 1)

        def sums_after(kt):
            return (kt - 2) // GRP - 1 if kt >= GRP + 2 and (kt - 2) % GRP == 0 else None

        def add_probs(dve, u, kt):
            j, m = divmod(kt, GRP)
            if m == 0:
                return
            for hp in range(2):
                hs = slice(2 * hp, 2 * hp + 2)
                dve.wait_ge(exps, START + NP * (u + 1) + 2 * kt + hp + 1)
                n = ADDS * (u + 1) + (ADDS // NG) * j + 2 * (m - 1) + hp
                out = part[:, j % 2, hs, :]
                rows = keys(kt)
                if m == 1:
                    dve.wait_ge(summed, START + NG * (u + 1) + max(0, j - 1))
                    nc.vector.tensor_tensor(out, prob[:, (kt - 1) % RING, hs, :], prob[:, kt % RING, hs, :],
                                            ALU.add).then_inc(added, 1)
                else:
                    dve.wait_ge(added, START + n - 1)
                    nc.vector.tensor_tensor(out[0:rows], out[0:rows], prob[0:rows, kt % RING, hs, :], ALU.add) \
                        .then_inc(added, 1)

        def tile_free(eng, u, kt, hp):
            eng.wait_ge(pv_done, START + NK * (u + 1) + kt - RING + 1)
            j, m = divmod(kt - RING, GRP)
            eng.wait_ge(added, START + ADDS * (u + 1) + (ADDS // NG) * j + 2 * max(0, m - 1) + hp + 1)

        def finish(dve, u, slot, use):
            dve.wait_ge(pv_done, START + NK * (u + 2))
            nc.vector.tensor_copy(out_sb[:], out_ps[:, 0:CW]).then_inc(out_copied, 1)
            dve.wait_ge(summed, START + NG * (u + 2))
            nc.vector.reciprocal(inv[:], sum_ps[:, 0:CW]).then_inc(sum_read, 1)
            dve.wait_ge(sum_read, START + 1 * (u + 1))
            dve.wait_ge(out_copied, START + 1 * (u + 1))
            dve.wait_ge(res_stored[slot], START + 16 * use)
            nc.vector.tensor_tensor(res[:, slot, :], out_sb[:], inv[:], ALU.mult).then_inc(res_done, 1)

        with nc.Block() as block:
            @block.sync
            def _(sp):
                for s in sems:
                    sp.sem_inc(s, START)

                branch(sp, lambda: loads(sp, NP), lambda: loads(sp, 2 * NP))

            @block.tensor
            def _(pe):
                image = []

                def fast():
                    def unit(g, u, slot, use, ahead):
                        for kt in range(NK):
                            for p in (2 * kt + 2, 2 * kt + 3):
                                if p < NP:
                                    if p >= SLOTS:
                                        pe.wait_ge(exps, START + NP * (u + 1) + p - SLOTS + 1)
                                    score_pair(g, slot, p)
                                else:
                                    if p == NP:
                                        nslot = 1 - slot
                                        pe.wait_ge(q_loaded[nslot], START + 64 * (use + 1 + (slot == 1)))
                                        if ahead is not None:
                                            pe.wait_ge(k_loaded[ahead], START + 64 * (image[0] + 1 + (ahead == 0)))
                                    pe.wait_ge(exps, START + NP * (u + 2) - 1 + (p - NP))
                                    score_pair(g if ahead is None else ahead, 1 - slot, p - NP)
                            if kt == 0:
                                pe.wait_ge(v_loaded[g], START + 16 * (image[0] + 1))
                            weighted_values(pe, u, g, kt)
                            j = sums_after(kt)
                            if j is not None:
                                row_sums(pe, u, j)
                        row_sums(pe, u, NG - 1)

                    pe.sem_inc(pv_done, NK)
                    pe.sem_inc(summed, NG)
                    pe.wait_ge(q_loaded[0], START + 64)
                    pe.wait_ge(k_loaded[0], START + 64)
                    score_pair(0, 0, 0)
                    score_pair(0, 0, 1)
                    with pe.Fori(0, B) as i:
                        b = Turn(pe, i)
                        image[:] = [b]
                        image_units(pe, b, unit)

                def exact():
                    def unit(g, u, slot, use, ahead):
                        pe.wait_ge(q_loaded[slot], START + 64 * (use + 1))
                        pe.wait_ge(k_loaded[g], START + 64 * (image[0] + 1))
                        pe.wait_ge(v_loaded[g], START + 16 * (image[0] + 1))
                        pe.wait_ge(shifted, START + NP * u)
                        for p in range(NP):
                            if p >= SLOTS:
                                pe.wait_ge(max_read, START + NP * u + p - SLOTS + 1)
                            score_pair(g, slot, p)
                        for p in range(NP):
                            if p >= SLOTS:
                                pe.wait_ge(shifted, START + NP * u + p - SLOTS + 1)
                            else:
                                pe.wait_ge(max_read, START + NP * (u + 1))
                            score_pair(g, slot, p)
                            if p % 2 and p > 2:
                                weighted_values(pe, u, g, p // 2 - 1)
                                j = sums_after(p // 2 - 1)
                                if j is not None:
                                    row_sums(pe, u, j)
                        weighted_values(pe, u, g, NK - 1)
                        row_sums(pe, u, NG - 1)

                    pe.sem_inc(pv_done, NK)
                    pe.sem_inc(summed, NG)
                    with pe.Fori(0, B) as i:
                        b = Turn(pe, i)
                        image[:] = [b]
                        image_units(pe, b, unit)

                branch(pe, fast, exact)

            @block.scalar
            def _(act):
                def fast():
                    def unit(g, u, slot, use, ahead):
                        for p in range(NP):
                            kt, hp = divmod(p, 2)
                            m = keys(kt)
                            act.wait_ge(scored, START + NP * u + p + 1)
                            tile_free(act, u, kt, hp)
                            nc.scalar.activation(prob[0:m, kt % RING, 2 * hp:2 * hp + 2, :],
                                                 scores[0:m, p % SLOTS, :, 0:CW], ACT.Exp, bias=-SHIFT) \
                                .then_inc(exps, 1)

                    act.sem_inc(exps, NP)
                    with act.Fori(0, B) as i:
                        b = Turn(act, i)
                        image_units(act, b, unit)

                def exact():
                    def unit(g, u, slot, use, ahead):
                        for p in range(NP):
                            kt, hp = divmod(p, 2)
                            m = keys(kt)
                            act.wait_ge(shifted, START + NP * u + p + 1)
                            tile = prob[0:m, kt % RING, 2 * hp:2 * hp + 2, :]
                            nc.scalar.activation(tile, tile, ACT.Exp).then_inc(exps, 1)

                    act.sem_inc(exps, NP)
                    with act.Fori(0, B) as i:
                        b = Turn(act, i)
                        image_units(act, b, unit)

                branch(act, fast, exact)

            @block.vector
            def _(dve):
                def fast():
                    def unit(g, u, slot, use, ahead):
                        for kt in range(NK):
                            add_probs(dve, u, kt)
                        finish(dve, u, slot, use)

                    dve.sem_inc(added, ADDS)
                    with dve.Fori(0, B) as i:
                        b = Turn(dve, i)
                        image_units(dve, b, unit)

                def exact():
                    def unit(g, u, slot, use, ahead):
                        for p in range(NP):
                            kt, hp = divmod(p, 2)
                            m = keys(kt)
                            src = scores[0:m, p % SLOTS, :, 0:CW]
                            hs = slice(2 * hp, 2 * hp + 2)
                            dve.wait_ge(scored, START + 2 * NP * u + p + 1)
                            if kt == 0:
                                nc.vector.tensor_copy(run_max[:, hs, :], src).then_inc(max_read, 1)
                            else:
                                dve.wait_ge(max_read, START + NP * u + p - 1)
                                nc.vector.tensor_tensor(run_max[0:m, hs, :], src, run_max[0:m, hs, :], ALU.max) \
                                    .then_inc(max_read, 1)
                        dve.wait_ge(max_all, START + 1 * (u + 1))
                        for p in range(NP + 2 * 2):
                            if p < NP:
                                kt, hp = divmod(p, 2)
                                m = keys(kt)
                                hs = slice(2 * hp, 2 * hp + 2)
                                dve.wait_ge(scored, START + 2 * NP * u + NP + p + 1)
                                tile_free(dve, u, kt, hp)
                                nc.vector.tensor_tensor(prob[0:m, kt % RING, hs, :], scores[0:m, p % SLOTS, :, 0:CW],
                                                        all_max[0:m, hs, :], ALU.subtract).then_inc(shifted, 1)
                            if p >= 4 and p % 2:
                                add_probs(dve, u, (p - 4) // 2)
                        finish(dve, u, slot, use)

                    dve.sem_inc(added, ADDS)
                    with dve.Fori(0, B) as i:
                        b = Turn(dve, i)
                        image_units(dve, b, unit)

                branch(dve, fast, exact)

            @block.gpsimd
            def _(pool):
                def exact():
                    with pool.Fori(0, B * U) as i:
                        u = Turn(pool, i)
                        pool.wait_ge(max_read, START + NP * (u + 1))
                        pool.wait_ge(shifted, START + NP * u)
                        pool.sem_inc(gate, 1)
                        nc.gpsimd.partition_all_reduce(all_max[:].rearrange("p h t -> p (h t)"),
                                                       run_max.rearrange("p h t -> p (h t)"), P,
                                                       bass.bass_isa.ReduceOp.max).then_inc(max_all, 1)

                ok = pool.value_load(k["bounded"][0:1, 0:1])
                with pool.If(ok < 1):
                    exact()


def part_c(nc, k, B, d, w_proj, Wf, bf, Wg, bg, Wh, bh, out):
    with ExitStack() as ctx:
        def sb(name, shape, dt=F32):
            return ctx.enter_context(nc.sbuf_tensor("c_" + name, shape, dt))

        sems = []

        def sem(name):
            sems.append(ctx.enter_context(nc.semaphore("c_" + name)))
            return sems[-1]

        bank = [ctx.enter_context(nc.psum_tensor(f"c_bank{i}", [P, 512], F32)) for i in range(8)]
        bank_p, bank_fg, bank_s, bank_h, bank_o = bank[0:2], bank[2], bank[3], bank[4:6], bank[6:8]
        CK = Wf.shape[1]
        att = sb("att", [P, G, T])
        yT = sb("yT", [P, CH, T])
        yn = sb("yn", [P, CH, T])
        y_nat = sb("y_nat", [TW, NT, C])
        fg = sb("fg", [CK, 2, 2, CW])
        sig = sb("sig", [TW, 2, TPC, TW])
        weights = sb("weights", [TW, 2, TPC, TW])
        h_sb = sb("h_sb", [TW, 2, TPC, C])
        z = sb("z", [TW, 2, TPC, C])
        wp = sb("wp", [P, CH, C])
        wfg = sb("wfg", [P, CH, 2 * CK])
        wh = sb("wh", [P, CH, C])
        bias_fg = sb("bias_fg", [2 * CK, 1])
        bias_h = sb("bias_h", [TW, 2, C])

        w_loaded = sem("w_loaded")
        x_loaded, att_loaded = sem("x_loaded"), sem("att_loaded")
        p_done, y_done, normed = sem("p_done"), sem("y_done"), sem("normed")
        tr_done, tr_read = sem("tr_done"), sem("tr_read")
        fg_done, fg_read, s_done, sig_done, masked = (sem("fg_done"), sem("fg_read"), sem("s_done"),
                                                      sem("sig_done"), sem("masked"))
        h_done, h_read, o_done, z_done = sem("h_done"), sem("h_read"), sem("o_done"), sem("z_done")
        z_stored = [sem(f"z_stored{s}") for s in range(2)]
        gn = GroupNorm(nc, sb, sem, k, bank_p[0])
        NP2 = NT // 2
        out_tok = out.rearrange("b h w c -> b (h w) c").rearrange("b (t p) c -> b p t c", p=TW)
        AHEAD = 3

        def slot_users(c):
            return max(0, c - 1)

        with nc.Block() as block:
            @block.sync
            def _(sp):
                for s in sems:
                    sp.sem_inc(s, START)

                def load(b):
                    sp.dma_start(att[:], d["att"][at(b)].rearrange("g p t -> p g t")).then_inc(att_loaded, 16)
                    sp.dma_start(yT[:], d["xT"][at(b)].rearrange("h p t -> p h t")).then_inc(x_loaded, 16)

                def store(b, c):
                    sp.wait_ge(z_done, START + NP2 * b + 2 * (c + 1))
                    sp.dma_start(out_tok[at(b), :, c * TPC:(c + 1) * TPC, :], z[:, c % 2]).then_inc(z_stored[c % 2], 16)

                def image(b, more):
                    if more:
                        sp.wait_ge(p_done, START + NP2 * (b + 1))
                        sp.wait_ge(normed, START + NP2 * (b + 1))
                        sp.wait_ge(tr_done, START + NP2 * (b + 1))
                        load(b + 1)
                    for c in range(NC):
                        store(b, c)

                load(0)
                sp.dma_start(wp[:], w_proj.rearrange("(h p) n -> p h n", p=P)).then_inc(w_loaded, 16)
                sp.dma_start(wfg[:, :, 0:CK], Wf.rearrange("(h p) n -> p h n", p=P)).then_inc(w_loaded, 16)
                sp.dma_start(wfg[:, :, CK:], Wg.rearrange("(h p) n -> p h n", p=P)).then_inc(w_loaded, 16)
                sp.dma_start(wh[:], Wh.rearrange("(h p) n -> p h n", p=P)).then_inc(w_loaded, 16)
                sp.dma_start(bias_fg[0:CK], bf.rearrange("(p a) -> p a", a=1)).then_inc(w_loaded, 16)
                sp.dma_start(bias_fg[CK:], bg.rearrange("(p a) -> p a", a=1)).then_inc(w_loaded, 16)
                for e in range(2):
                    sp.dma_start(bias_h[:, e, :], bh.rearrange("(a n) -> a n", a=1).broadcast_to([TW, C])) \
                        .then_inc(w_loaded, 16)
                with sp.Fori(0, B - 1) as i:
                    b = Turn(sp, i)
                    image(b, True)
                image(B - 1, False)
                sp.wait_ge(z_stored[0], START + 16 * ((NC + 1) // 2) * B)
                sp.wait_ge(z_stored[1], START + 16 * (NC // 2) * B)

            @block.tensor
            def _(pe):
                def project(b):
                    pe.wait_ge(att_loaded, START + 16 * (b + 1))
                    for i in range(CH * NC):
                        c, ch = divmod(i, CH)
                        pe.wait_ge(y_done, START + NP2 * b + max(0, i - 1))
                        for g in range(G):
                            last = nc.tensor.matmul(bank_p[ch][:, 0:CW], wp[:, g, ch * P:(ch + 1) * P],
                                                    att[:, g, c * CW:(c + 1) * CW], start=g == 0, stop=g == G - 1)
                        last.then_inc(p_done, 1)

                def average_means(b):
                    pe.wait_ge(y_done, START + NP2 * (b + 1))
                    gn.average_means(pe, b)

                def transposes(b):
                    pe.wait_ge(y_done, START + NP2 * (b + 1))
                    for i in range(NP2):
                        if i < 2:
                            pe.wait_ge(z_done, START + NP2 * b)
                        else:
                            pe.wait_ge(tr_read, START + NP2 * b + i - 1)
                        for e in range(2):
                            for ch in range(CH):
                                t = 2 * i + e
                                last = nc.tensor.transpose(bank_o[i % 2][0:TW, e * C + ch * P:e * C + (ch + 1) * P],
                                                           yT[:, ch, t * TW:(t + 1) * TW], k["ident"][:])
                        last.then_inc(tr_done, 1)

                def f_g_h_scores(b, c):
                    pe.wait_ge(normed, START + CH * (NC * b + c + 1))
                    pe.wait_ge(fg_read, START + 2 * (NC * b + c))
                    for ch in range(CH):
                        last = nc.tensor.matmul(bank_fg[0:2 * CK, 0:CW], wfg[:, ch, :], yn[:, ch, c * CW:(c + 1) * CW],
                                                start=ch == 0, stop=ch == CH - 1)
                    last.then_inc(fg_done, 1)
                    for e in range(2):
                        pe.wait_ge(h_read, START + NP2 * b + max(0, 2 * c + e - 1))
                        for t in range(2):
                            first = (c * TPC + 2 * e + t) * TW
                            for ch in range(CH):
                                last = nc.tensor.matmul(bank_h[e][0:TW, t * C:(t + 1) * C], yn[:, ch, first:first + TW],
                                                        wh[:, ch, :], start=ch == 0, stop=ch == CH - 1)
                        last.then_inc(h_done, 1)
                    pe.wait_ge(fg_read, START + 2 * (NC * b + c + 1))
                    pe.wait_ge(sig_done, START + NC * b + c)
                    for t in range(TPC):
                        ts = slice(t * TW, (t + 1) * TW)
                        last = nc.tensor.matmul(bank_s[0:TW, ts], fg[:, c % 2, 1, ts], fg[:, c % 2, 0, ts],
                                                start=True, stop=True)
                    last.then_inc(s_done, 1)

                def weighted_h(b, c):
                    pe.wait_ge(masked, START + NC * b + c + 1)
                    pe.wait_ge(h_read, START + NP2 * b + 2 * (c + 1))
                    for e in range(2):
                        i = 2 * c + e
                        if i < 2:
                            pe.wait_ge(tr_read, START + NP2 * (b + 1))
                        else:
                            pe.wait_ge(z_done, START + NP2 * b + i - 1)
                        for t in range(2):
                            last = nc.tensor.matmul(bank_o[e][0:TW, t * C:(t + 1) * C],
                                                    weights[:, c % 2, 2 * e + t, :], h_sb[:, c % 2, 2 * e + t, :],
                                                    start=True, stop=True)
                        last.then_inc(o_done, 1)

                def image(b, more):
                    transposes(b)
                    for c in range(NC):
                        f_g_h_scores(b, c)
                        if c:
                            weighted_h(b, c - 1)
                        if more and c == AHEAD:
                            project(b + 1)
                        if more and c == AHEAD + 1:
                            average_means(b + 1)
                        if more and c == AHEAD + 2:
                            gn.average_spread(pe, b + 1)
                    weighted_h(b, NC - 1)

                pe.wait_ge(w_loaded, START + 16 * 8)
                project(0)
                average_means(0)
                gn.average_spread(pe, 0)
                with pe.Fori(0, B - 1) as i:
                    b = Turn(pe, i)
                    image(b, True)
                image(B - 1, False)

            @block.scalar
            def _(act):
                def image(b):
                    act.wait_ge(z_done, START + NP2 * b)
                    for i in range(NP2):
                        act.wait_ge(tr_done, START + NP2 * b + i + 1)
                        nc.scalar.copy(y_nat[:, 2 * i:2 * i + 2, :],
                                       bank_o[i % 2][0:TW, :].rearrange("p (t c) -> p t c", c=C)).then_inc(tr_read, 1)
                    for c in range(NC):
                        act.wait_ge(fg_done, START + NC * b + c + 1)
                        act.wait_ge(s_done, START + NC * b + slot_users(c))
                        for n in range(2):
                            nc.scalar.activation(fg[:, c % 2, n, :], bank_fg[n * CK:(n + 1) * CK, 0:CW], ACT.Identity,
                                                 bias=bias_fg[n * CK:(n + 1) * CK, :]).then_inc(fg_read, 1)
                        act.wait_ge(s_done, START + NC * b + c + 1)
                        act.wait_ge(masked, START + NC * b + slot_users(c))
                        nc.scalar.activation(sig[:, c % 2].rearrange("p t n -> p (t n)"), bank_s[0:TW, 0:CW],
                                             ACT.Sigmoid).then_inc(sig_done, 1)

                act.wait_ge(w_loaded, START + 16 * 8)
                with act.Fori(0, B) as i:
                    b = Turn(act, i)
                    image(b)

            @block.gpsimd
            def _(pool):
                def image(b, more):
                    for c in range(NC):
                        pool.wait_ge(sig_done, START + NC * b + c + 1)
                        pool.wait_ge(o_done, START + NP2 * b + 2 * slot_users(c))
                        nc.gpsimd.tensor_tensor(weights[:, c % 2], sig[:, c % 2],
                                                k["row_mask"][0:TW, None, :].broadcast_to([TW, TPC, TW]),
                                                ALU.mult).then_inc(masked, 1)
                        if more and c == AHEAD + 2:
                            gn.rstd(pool, b + 1)

                gn.rstd(pool, 0)
                with pool.Fori(0, B - 1) as i:
                    b = Turn(pool, i)
                    image(b, True)
                image(B - 1, False)

            @block.vector
            def _(dve):
                v = nc.vector

                def add_residual(b):
                    dve.wait_ge(x_loaded, START + 16 * (b + 1))
                    for i in range(CH * NC):
                        c, ch = divmod(i, CH)
                        s = yT[:, ch, c * CW:(c + 1) * CW]
                        dve.wait_ge(p_done, START + NP2 * b + i + 1)
                        v.tensor_tensor(s, bank_p[ch][:, 0:CW], s, ALU.add).then_inc(y_done, 1)
                        if i:
                            dve.wait_ge(y_done, START + NP2 * b + i)
                            gn.stats(yT, *divmod(i - 1, CH))
                    dve.wait_ge(y_done, START + NP2 * (b + 1))
                    gn.stats(yT, NC - 1, CH - 1)
                    gn.aggregate(dve, b)

                def norm(b):
                    dve.wait_ge(gn.rstd_done, START + 1 * (b + 1))
                    dve.wait_ge(h_done, START + NP2 * b)
                    for c in range(NC):
                        for ch in range(CH):
                            gn.norm(yn, yT, c, ch).then_inc(normed, 1)

                def h_rows(b, c):
                    dve.wait_ge(o_done, START + NP2 * b + 2 * slot_users(c))
                    for e in range(2):
                        dve.wait_ge(h_done, START + NP2 * b + 2 * c + e + 1)
                        v.tensor_tensor(h_sb[:, c % 2, 2 * e:2 * e + 2, :],
                                        bank_h[e][0:TW, :].rearrange("p (t c) -> p t c", c=C), bias_h[:], ALU.add) \
                            .then_inc(h_read, 1)

                def results(b, c):
                    users = (NC + 1) // 2 if c % 2 == 0 else NC // 2
                    dve.wait_ge(z_stored[c % 2], START + 16 * (users * b + c // 2))
                    for e in range(2):
                        t = TPC * c + 2 * e
                        dve.wait_ge(o_done, START + NP2 * b + 2 * c + e + 1)
                        v.tensor_tensor(z[:, c % 2, 2 * e:2 * e + 2, :],
                                        bank_o[e][0:TW, :].rearrange("p (t c) -> p t c", c=C),
                                        y_nat[:, t:t + 2, :], ALU.add).then_inc(z_done, 1)

                def image(b, more):
                    norm(b)
                    dve.wait_ge(tr_read, START + NP2 * (b + 1))
                    for c in range(NC):
                        h_rows(b, c)
                        if c:
                            results(b, c - 1)
                        if more and c == AHEAD:
                            add_residual(b + 1)
                        if more and c == AHEAD + 1:
                            gn.spread(dve, b + 1)
                        if more and c == AHEAD + 2:
                            gn.variance(dve, b + 1)
                    results(b, NC - 1)

                dve.wait_ge(w_loaded, START + 16 * 8)
                add_residual(0)
                gn.spread(dve, 0)
                gn.variance(dve, 0)
                with dve.Fori(0, B - 1) as i:
                    b = Turn(dve, i)
                    image(b, True)
                image(B - 1, False)


def build(nc, x, w_qkv, w_proj, Wf, bf, Wg, bg, Wh, bh, out):
    B = x.shape[0]
    nc.disable_value_cache = True
    d = dict(
        xT=nc.dram_tensor("xT_scratch", (B, CH, P, T), F32).ap(),
        q=nc.dram_tensor("q_scratch", (B, G, 2, P, T), F32).ap(),
        k=nc.dram_tensor("k_scratch", (B, G, 2, P, T), F32).ap(),
        v=nc.dram_tensor("v_scratch", (B, G, P, NK, P), F32).ap(),
        att=nc.dram_tensor("att_scratch", (B, G, P, T), F32).ap(),
    )
    with ExitStack() as ctx:
        k = build_consts(nc, ctx)
        part_a(nc, k, B, x, w_qkv, d)
        part_b(nc, k, B, d)
        part_c(nc, k, B, d, w_proj, Wf, bf, Wg, bg, Wh, bh, out)


_INS = ["x", "L0_conv_w_qkv", "L0_conv_w_proj", "L1_conv_Wf", "L1_conv_bf", "L1_conv_Wg", "L1_conv_bg",
        "L1_conv_Wh", "L1_conv_bh"]


def kernel(**inputs):
    import numpy as _np
    import concourse.bacc as _bacc
    from concourse import mybir as _mybir
    from concourse.bass_utils import run_bass_kernel_spmd as _run

    nc = _bacc.Bacc("TRN2", target_bir_lowering=False, num_devices=1)
    arrays, args = {}, []
    for name in _INS:
        a = _np.ascontiguousarray(inputs[name])
        arrays[f"in_{name}"] = a
        args.append(nc.dram_tensor(f"in_{name}", a.shape, _mybir.dt.from_np(a.dtype), kind="ExternalInput").ap())
    out = nc.dram_tensor("out_y", inputs["x"].shape, _mybir.dt.float32, kind="ExternalOutput").ap()
    build(nc, *args, out)
    return _run(nc, [arrays], core_ids=[0]).results[0]["out_y"]
```

```python
from contextlib import ExitStack

import concourse.bass as bass
from concourse import mybir

F32 = mybir.dt.float32
F32R = mybir.dt.float32r
BF16 = mybir.dt.bfloat16
I32 = mybir.dt.int32
ACT = mybir.ActivationFunctionType
ALU = mybir.AluOpType
AX = mybir.AxisListType

P = 128
C = 256
CH = C // P
SIDE = 56
T = SIDE * SIDE
HD = 32
HG = 4
G = 2
CW = 448
NC = T // CW
TW = 2 * SIDE
TPC = CW // TW
NT = T // TW
NK = (T + P - 1) // P
KLAST = T - (NK - 1) * P
GSIZE = C // 32
EPS = 1e-5
SCALE = float(HD) ** -0.25

SHIFT = 40.0
SCORE_BOUND = 100.0
MEAN_BOUND = 10.0
WV_BOUND = 1e3
SLACK = 1.02


def keys(kt):
    return KLAST if kt == NK - 1 else P


def build_consts(nc, ctx):
    def sb(name, shape, dt=F32):
        return ctx.enter_context(nc.sbuf_tensor(name, shape, dt))

    k = dict(
        ident=sb("ident", [P, P]),
        group_avg=sb("group_avg", [P, P]),
        head_sum=sb("head_sum", [P, P]),
        head_sum_bf=sb("head_sum_bf", [P, P], BF16),
        ones=sb("ones", [P, HD]),
        minus_half=sb("minus_half", [P, CH]),
        row_mask=sb("row_mask", [TW, TW]),
        norm_max=sb("norm_max", [P, 4, 4]),
        xn_mean=sb("xn_mean", [P, CH, 4]),
        bounded=sb("bounded", [P, 1], I32),
    )
    made = ctx.enter_context(nc.semaphore("consts_made"))
    count = [0]
    with nc.Block() as block:
        @block.gpsimd
        def _(pool):
            def step(ins):
                ins.then_inc(made, 1)
                count[0] += 1
                pool.wait_ge(made, count[0])

            def blocks(t, value, width):
                n = t.shape[1] // width
                v = t[:].rearrange("p (n w) -> p n w", w=width)
                step(nc.gpsimd.memset(t[:], value))
                step(nc.gpsimd.affine_select(out=v, in_=v, compare_op=ALU.is_ge, fill=0.0, base=0,
                                             pattern=[[-width, n], [0, width]], channel_multiplier=1))
                step(nc.gpsimd.affine_select(out=v, in_=v, compare_op=ALU.is_ge, fill=0.0, base=width - 1,
                                             pattern=[[width, n], [0, width]], channel_multiplier=-1))

            step(nc.gpsimd.memset(k["ident"][:], 0.0))
            step(nc.gpsimd.affine_select(out=k["ident"][:], in_=k["ident"][:], compare_op=ALU.not_equal, fill=1.0,
                                         base=0, pattern=[[-1, P]], channel_multiplier=1))
            blocks(k["group_avg"], 1.0 / GSIZE, GSIZE)
            blocks(k["head_sum"], 1.0, HD)
            blocks(k["row_mask"], 1.0, SIDE)
            step(nc.gpsimd.tensor_copy(k["head_sum_bf"][:], k["head_sum"][:]))
            step(nc.gpsimd.memset(k["ones"][:], 1.0))
            step(nc.gpsimd.memset(k["minus_half"][:], -0.5))
    return k


START = 1


class Turn:

    def __init__(self, eng, value, offset=0, kept=None):
        self.eng, self.value, self.offset = eng, value, offset
        self.kept = {} if kept is None else kept

    def __mul__(self, n):
        if isinstance(self.value, int):
            return (self.value + self.offset) * n
        if n not in self.kept:
            self.kept[n] = self.eng.snap(self.value * n)
        return self.kept[n] + self.offset * n

    __rmul__ = __mul__

    def __add__(self, n):
        return Turn(self.eng, self.value, self.offset + n, self.kept)


def at(turn):
    return turn.value + turn.offset if isinstance(turn, Turn) else turn


class GroupNorm:

    def __init__(self, nc, sb, sem, k, psum):
        self.nc, self.k, self.psum = nc, k, psum
        self.chunk_stats = sb("chunk_stats", [P, CH, NC, 6])
        self.moments = sb("moments", [P, CH, 2])
        self.off = sb("off", [P, CH])
        self.spread_t = sb("spread", [P, CH])
        self.mean = sb("mean", [P, CH])
        self.var = sb("var", [P, CH])
        self.rstd_t = sb("rstd", [P, CH])
        self.stat_done = sem("stat_done")
        self.aggregated = sem("aggregated")
        self.means_avg = sem("means_avg")
        self.spread_done = sem("spread_done")
        self.spread_avg = sem("spread_avg")
        self.var_done = sem("var_done")
        self.rstd_done = sem("rstd_done")
        self.gate = sem("gate")

    def stats(self, src, c, ch):
        self.nc.vector.bn_stats(self.chunk_stats[:, ch, c, :],
                                src[:, ch, c * CW:(c + 1) * CW]).then_inc(self.stat_done, 1)

    def aggregate(self, dve, b):
        dve.wait_ge(self.stat_done, START + CH * NC * (b + 1))
        dve.sem_inc(self.gate, 1)
        for ch in range(CH):
            self.nc.vector.bn_aggr(self.moments[:, ch, :], self.chunk_stats[:, ch, :, :]) \
                .then_inc(self.aggregated, 1)

    def average_means(self, pe, b):
        pe.wait_ge(self.aggregated, START + CH * (b + 1))
        self.nc.tensor.matmul(self.psum[:, 0:CH], self.k["group_avg"][:], self.moments[:, :, 0],
                              start=True, stop=True).then_inc(self.means_avg, 1)

    def spread(self, dve, b):
        v = self.nc.vector
        dve.wait_ge(self.means_avg, START + 1 * (b + 1))
        v.tensor_copy(self.mean[:], self.psum[:, 0:CH]).then_inc(self.spread_done, 1)
        dve.wait_ge(self.spread_done, START + 3 * b + 1)
        v.tensor_tensor(self.off[:], self.moments[:, :, 0], self.mean[:], ALU.subtract) \
            .then_inc(self.spread_done, 1)
        dve.wait_ge(self.spread_done, START + 3 * b + 2)
        v.tensor_tensor(self.spread_t[:], self.off[:], self.off[:], ALU.mult).then_inc(self.spread_done, 1)
        dve.wait_ge(self.spread_done, START + 3 * b + 3)
        v.tensor_tensor(self.var[:], self.spread_t[:], self.moments[:, :, 1], ALU.add) \
            .then_inc(self.var_done, 1)

    def average_spread(self, pe, b):
        pe.wait_ge(self.var_done, START + 2 * b + 1)
        self.nc.tensor.matmul(self.psum[:, CH:2 * CH], self.k["group_avg"][:], self.var[:],
                              start=True, stop=True).then_inc(self.spread_avg, 1)

    def variance(self, dve, b):
        dve.wait_ge(self.spread_avg, START + 1 * (b + 1))
        self.nc.vector.tensor_scalar(self.spread_t[:], self.psum[:, CH:2 * CH], EPS, None, ALU.add) \
            .then_inc(self.var_done, 1)

    def rstd(self, pool, b):
        pool.wait_ge(self.var_done, START + 2 * b + 2)
        self.nc.gpsimd.tensor_tensor(self.rstd_t[:], self.spread_t[:], self.k["minus_half"][:], ALU.pow) \
            .then_inc(self.rstd_done, 1)

    def norm(self, dst, src, c, ch):
        s = slice(c * CW, (c + 1) * CW)
        return self.nc.vector.tensor_scalar(dst[:, ch, s], src[:, ch, s], self.mean[:, ch:ch + 1],
                                            self.rstd_t[:, ch:ch + 1], ALU.subtract, ALU.mult)


def part_a(nc, k, B, x, w_qkv, d):
    PR = 2 * NC
    SR = NC
    NQ = 4 * NC
    with ExitStack() as ctx:
        def sb(name, shape, dt=F32):
            return ctx.enter_context(nc.sbuf_tensor("a_" + name, shape, dt))

        sems = []

        def sem(name):
            sems.append(ctx.enter_context(nc.semaphore("a_" + name)))
            return sems[-1]

        bank = [ctx.enter_context(nc.psum_tensor(f"a_bank{i}", [P, 512], F32)) for i in range(8)]
        bank_t, bank_q, bank_n, bank_v = bank[0:2], bank[2:5], bank[5], bank[6:8]
        x_in = sb("x_in", [TW, NT, C])
        xT = sb("xT", [P, CH, T])
        xn = sb("xn", [P, CH, T])
        w = sb("w", [P, CH, 3 * C])
        parts = sb("parts", [P, PR, 2, CW], F32R)
        square = sb("square", [P, SR, CW], BF16)
        v_st = sb("v_st", [P, G, NK, HG * HD])
        item_max = sb("item_max", [P, NQ])
        kmean2 = sb("kmean2", [P, G * B])
        bound = sb("bound", [P, 2 * G * B + 1])
        worst = sb("worst", [P, 2])

        w_loaded, x_stored, v_stored = sem("w_loaded"), sem("x_stored"), sem("v_stored")
        x_loaded = [sem(f"x_loaded{c}") for c in range(NC)]
        part_stored = [sem(f"part_stored{n}") for n in range(PR)]
        t_done, t_act, t_dve = sem("t_done"), sem("t_act"), sem("t_dve")
        normed = sem("normed")
        q_done, q_high, q_low = sem("q_done"), sem("q_high"), sem("q_low")
        squared, summed, max_taken = sem("squared"), sem("summed"), sem("max_taken")
        v_done, v_act, v_dve, v_zero = sem("v_done"), sem("v_act"), sem("v_dve"), sem("v_zero")
        end_pe, end_dve, end_pool, image_max = sem("end_pe"), sem("end_dve"), sem("end_pool"), sem("image_max")
        mean_saved = sem("mean_saved")
        gn = GroupNorm(nc, sb, sem, k, bank_n)
        x_tok = x.rearrange("b h w c -> b (h w) c").rearrange("b (t p) c -> b p t c", p=TW)
        VA, VD = (NK + 1) // 2, NK // 2

        with nc.Block() as block:
            @block.sync
            def _(sp):
                for s in sems:
                    sp.sem_inc(s, START)

                def load_x(b, c):
                    sp.dma_start(x_in[:, c * TPC:(c + 1) * TPC, :], x_tok[at(b), :, c * TPC:(c + 1) * TPC, :]) \
                        .then_inc(x_loaded[c], 16)

                def image(b, more):
                    sp.wait_ge(t_act, START + NC * (b + 1))
                    sp.wait_ge(t_dve, START + NC * (b + 1))
                    sp.dma_start(d["xT"][at(b)].rearrange("h p t -> p h t"), xT[:]).then_inc(x_stored, 16)
                    if more:
                        for c in range(NC):
                            load_x(b + 1, c)
                    for c in range(NC):
                        for j in range(4):
                            dst = d["q" if j < 2 else "k"][at(b), j % 2]
                            n = (4 * c + j) % PR
                            sp.wait_ge(q_low, START + NQ * b + 4 * c + j + 1)
                            sp.dma_start(dst[:, :, c * CW:(c + 1) * CW].rearrange("s p t -> p s t"),
                                         parts[:, n].bitcast(F32)).then_inc(part_stored[n], 16)
                    sp.wait_ge(v_act, START + VA * (b + 1))
                    sp.wait_ge(v_dve, START + VD * (b + 1))
                    sp.dma_start(d["v"][at(b)].rearrange("g p k n -> p g k n"), v_st[:]).then_inc(v_stored, 16)

                for c in range(NC):
                    load_x(0, c)
                    if c == 0:
                        sp.dma_start(w[:], w_qkv.rearrange("(h p) n -> p h n", p=P)).then_inc(w_loaded, 16)
                with sp.Fori(0, B - 1) as i:
                    b = Turn(sp, i)
                    image(b, True)
                image(B - 1, False)
                sp.wait_ge(x_stored, START + 16 * B)
                sp.wait_ge(v_stored, START + 16 * B)
                for n in range(PR):
                    sp.wait_ge(part_stored[n], START + 16 * (NQ // PR) * B)

            @block.tensor
            def _(pe):
                def transposes(b):
                    for c in range(NC):
                        pe.wait_ge(x_loaded[c], START + 16 * (b + 1))
                        for ch, freed in ((0, t_act), (1, t_dve)):
                            if not (isinstance(b, int) and b == 0 and c == 0):
                                pe.wait_ge(freed, START + NC * b + c)
                            for t in range(TPC):
                                last = nc.tensor.transpose(bank_t[ch][:, t * TW:(t + 1) * TW],
                                                           x_in[:, c * TPC + t, ch * P:(ch + 1) * P],
                                                           k["ident"][0:TW, 0:TW])
                            last.then_inc(t_done, 1)

                def head_norms(b, i):
                    pe.wait_ge(squared, START + NQ * b + i + 1)
                    pe.wait_ge(max_taken, START + NQ * b + i)
                    nc.tensor.matmul(bank_n[:, 0:CW], k["head_sum_bf"][:], square[:, i % SR, :],
                                     start=True, stop=True).then_inc(summed, 1)

                def q_and_k(b):
                    for i in range(NQ):
                        c, j = divmod(i, 4)
                        if j == 0:
                            pe.wait_ge(normed, START + CH * (NC * b + c + 1))
                        pe.wait_ge(q_low, START + NQ * b + max(0, i - 2))
                        for ch in range(CH):
                            last = nc.tensor.matmul(bank_q[i % 3][:, 0:CW], w[:, ch, j * P:(j + 1) * P],
                                                    xn[:, ch, c * CW:(c + 1) * CW],
                                                    start=ch == 0, stop=ch == CH - 1)
                        last.then_inc(q_done, 1)
                        if i >= 3:
                            head_norms(b, i - 3)
                    for i in range(NQ - 3, NQ):
                        head_norms(b, i)

                def values(b, more):
                    for kt in range(NK):
                        freed, n = (v_dve, VD) if kt % 2 else (v_act, VA)
                        pe.wait_ge(freed, START + n * b + kt // 2)
                        m = keys(kt)
                        for ch in range(CH):
                            last = nc.tensor.matmul(bank_v[kt % 2][0:m, 0:C], xn[:, ch, kt * P:kt * P + m],
                                                    w[:, ch, 2 * C:3 * C], start=ch == 0, stop=ch == CH - 1)
                        last.then_inc(v_done, 1)
                        if more and kt == 10:
                            pe.wait_ge(max_taken, START + NQ * (b + 1))
                            gn.average_means(pe, b + 1)
                        if more and kt == 17:
                            gn.average_spread(pe, b + 1)

                pe.wait_ge(w_loaded, START + 16)
                transposes(0)
                gn.average_means(pe, 0)
                gn.average_spread(pe, 0)
                with pe.Fori(0, B - 1) as i:
                    b = Turn(pe, i)
                    q_and_k(b)
                    transposes(b + 1)
                    values(b, True)
                q_and_k(B - 1)
                values(B - 1, False)
                pe.wait_ge(mean_saved, START + B)
                pe.wait_ge(max_taken, START + NQ * B)
                for g in range(G):
                    for ch in range(CH):
                        last = nc.tensor.matmul(bank_n[:, g * B:(g + 1) * B],
                                                w[:, ch, C + g * P:C + (g + 1) * P], k["xn_mean"][:, ch, 0:B],
                                                start=ch == 0, stop=ch == CH - 1)
                last.then_inc(end_pe, 1)
                pe.wait_ge(end_dve, START + 2)
                nc.tensor.matmul(bank_q[0][:, 0:G * B], k["head_sum"][:], kmean2[:], start=True, stop=True) \
                    .then_inc(end_pe, 1)

            @block.scalar
            def _(act):
                def evacuate_x(b):
                    for c in range(NC):
                        if c == 0 and not isinstance(b, int):
                            act.wait_ge(normed, START + CH * NC * b)
                            act.wait_ge(x_stored, START + 16 * b)
                        act.wait_ge(t_done, START + CH * (NC * b + c) + 1)
                        nc.scalar.copy(xT[:, 0, c * CW:(c + 1) * CW], bank_t[0][:, 0:CW]).then_inc(t_act, 1)

                def high_parts(b):
                    for i in range(NQ):
                        n = i % PR
                        act.wait_ge(q_done, START + NQ * b + i + 1)
                        act.wait_ge(part_stored[n], START + 16 * ((NQ // PR) * b + i // PR))
                        if i >= PR:
                            act.wait_ge(squared, START + NQ * b + i - PR + 1)
                        nc.scalar.activation(parts[:, n, 0, :], bank_q[i % 3][:, 0:CW], ACT.Copy, scale=SCALE) \
                            .then_inc(q_high, 1)

                def evacuate_v(b):
                    act.wait_ge(v_stored, START + 16 * b)
                    for kt in range(0, NK, 2):
                        m = keys(kt)
                        act.wait_ge(v_done, START + NK * b + kt + 1)
                        nc.scalar.copy(v_st[0:m, :, kt, :], bank_v[0][0:m, 0:C].rearrange("p (g n) -> p g n", g=G)) \
                            .then_inc(v_act, 1)

                evacuate_x(0)
                act.wait_ge(v_zero, START + 1)
                with act.Fori(0, B - 1) as i:
                    b = Turn(act, i)
                    high_parts(b)
                    evacuate_x(b + 1)
                    evacuate_v(b)
                high_parts(B - 1)
                evacuate_v(B - 1)

            @block.gpsimd
            def _(pool):
                def squares(b):
                    for i in range(NQ):
                        pool.wait_ge(q_high, START + NQ * b + i + 1)
                        pool.wait_ge(summed, START + NQ * b + max(0, i - SR + 1))
                        high = parts[:, i % PR, 0, :].bitcast(F32)
                        nc.gpsimd.tensor_tensor(square[:, i % SR, :], high, high, ALU.mult).then_inc(squared, 1)

                nc.gpsimd.memset(v_st[KLAST:P, :, NK - 1, :], 0.0).then_inc(v_zero, 1)
                pool.wait_ge(v_zero, START + 1)
                gn.rstd(pool, 0)
                with pool.Fori(0, B - 1) as i:
                    b = Turn(pool, i)
                    squares(b)
                    pool.wait_ge(normed, START + CH * NC * (b + 1))
                    gn.rstd(pool, b + 1)
                squares(B - 1)
                pool.wait_ge(end_dve, START + 3 + 4)
                nc.gpsimd.partition_all_reduce(worst[:, 1:2], worst[:, 0:1], P, bass.bass_isa.ReduceOp.max) \
                    .then_inc(end_pool, 1)

            @block.vector
            def _(dve):
                v = nc.vector

                def evacuate_x(b):
                    for c in range(NC):
                        if c == 0 and not isinstance(b, int):
                            dve.wait_ge(normed, START + CH * NC * b)
                            dve.wait_ge(x_stored, START + 16 * b)
                        dve.wait_ge(t_done, START + CH * (NC * b + c + 1))
                        v.tensor_copy(xT[:, 1, c * CW:(c + 1) * CW], bank_t[1][:, 0:CW]).then_inc(t_dve, 1)
                        dve.wait_ge(t_act, START + NC * b + c + 1)
                        gn.stats(xT, c, 0)
                        dve.wait_ge(t_dve, START + NC * b + c + 1)
                        gn.stats(xT, c, 1)

                def norm(b):
                    dve.wait_ge(gn.rstd_done, START + 1 * (b + 1))
                    v.tensor_tensor(k["xn_mean"][:, :, at(b)], gn.off[:], gn.rstd_t[:], ALU.mult) \
                        .then_inc(mean_saved, 1)
                    dve.wait_ge(v_done, START + NK * b)
                    for c in range(NC):
                        for ch in range(CH):
                            gn.norm(xn, xT, c, ch).then_inc(normed, 1)

                def take_max(b, i):
                    dve.wait_ge(summed, START + NQ * b + i + 1)
                    v.reduce_max(item_max[:, i:i + 1], bank_n[:, 0:CW], AX.X).then_inc(max_taken, 1)

                def low_parts(b):
                    for i in range(NQ):
                        n = i % PR
                        dve.wait_ge(q_high, START + NQ * b + i + 1)
                        v.scalar_tensor_tensor(out=parts[:, n, 1, :], in0=bank_q[i % 3][:, 0:CW], scalar=SCALE,
                                               in1=parts[:, n, 0, :].bitcast(F32), op0=ALU.mult,
                                               op1=ALU.subtract).then_inc(q_low, 1)
                        if i >= 3:
                            take_max(b, i - 3)
                    for i in range(NQ - 3, NQ):
                        take_max(b, i)
                    dve.wait_ge(max_taken, START + NQ * (b + 1))
                    v.tensor_reduce(k["norm_max"][:, at(b), :], item_max[:].rearrange("p (c j) -> p j c", j=4),
                                    AX.X, ALU.max).then_inc(image_max, 1)

                def values(b, more):
                    dve.wait_ge(v_stored, START + 16 * b)
                    if more:
                        gn.aggregate(dve, b + 1)
                    for kt in range(1, NK, 2):
                        dve.wait_ge(v_done, START + NK * b + kt + 1)
                        v.tensor_copy(v_st[:, :, kt, :], bank_v[1][:, 0:C].rearrange("p (g n) -> p g n", g=G)) \
                            .then_inc(v_dve, 1)
                        if more and kt == 13:
                            gn.spread(dve, b + 1)
                        if more and kt == 21:
                            gn.variance(dve, b + 1)

                evacuate_x(0)
                gn.aggregate(dve, 0)
                gn.spread(dve, 0)
                gn.variance(dve, 0)
                with dve.Fori(0, B - 1) as i:
                    b = Turn(dve, i)
                    norm(b)
                    low_parts(b)
                    dve.wait_ge(image_max, START + 1 * (b + 1))
                    evacuate_x(b + 1)
                    values(b, True)
                norm(B - 1)
                low_parts(B - 1)
                values(B - 1, False)

                n = G * B
                dve.wait_ge(end_pe, START + 1)
                v.tensor_scalar(kmean2[:], bank_n[:, 0:n], SCALE, None, ALU.mult).then_inc(end_dve, 1)
                dve.wait_ge(end_dve, START + 1)
                v.tensor_tensor(kmean2[:], kmean2[:], kmean2[:], ALU.mult).then_inc(end_dve, 1)
                dve.wait_ge(image_max, START + B)
                q2 = k["norm_max"][:, 0:B, 0:G]
                k2 = k["norm_max"][:, 0:B, G:2 * G]
                v.scalar_tensor_tensor(out=bound[:, 0:n].rearrange("p (b g) -> p b g", g=G), in0=q2,
                                       scalar=(SLACK / SCORE_BOUND) ** 2, in1=k2, op0=ALU.mult, op1=ALU.mult) \
                    .then_inc(end_dve, 1)
                dve.wait_ge(end_pe, START + 2)
                v.scalar_tensor_tensor(out=bound[:, n:2 * n].rearrange("p (b g) -> p b g", g=G), in0=q2,
                                       scalar=(SLACK / MEAN_BOUND) ** 2,
                                       in1=bank_q[0][:, 0:n].rearrange("p (g b) -> p b g", g=G),
                                       op0=ALU.mult, op1=ALU.mult).then_inc(end_dve, 1)
                v.tensor_reduce(worst[:, 0:1], w[:, :, 2 * C:3 * C], AX.XY, ALU.max, apply_absolute_value=True) \
                    .then_inc(end_dve, 1)
                dve.wait_ge(end_dve, START + 5)
                v.tensor_scalar(bound[:, 2 * n:2 * n + 1], worst[:, 0:1], 1.0 / WV_BOUND, None, ALU.mult) \
                    .then_inc(end_dve, 1)
                dve.wait_ge(end_dve, START + 6)
                v.reduce_max(worst[:, 0:1], bound[:, 0:2 * n + 1], AX.X).then_inc(end_dve, 1)
                dve.wait_ge(end_pool, START + 1)
                v.tensor_scalar(k["bounded"][:], worst[:, 1:2], 1.0, None, ALU.is_le).then_inc(end_dve, 1)


def part_b(nc, k, B, d):
    NP = 2 * NK
    U = G * NC
    SLOTS = 3
    RING = 5
    NG = 3
    GROUP = [NK // NG * j for j in range(NG)] + [NK]
    ADDS = 2 * (NK - NG)
    AHEAD = 6
    PIECE = [0, 3, 6, 12, 18, NK]
    PIECES = len(PIECE) - 1
    with ExitStack() as ctx:
        def sb(name, shape, dt=F32):
            return ctx.enter_context(nc.sbuf_tensor("b_" + name, shape, dt))

        sems = []

        def sem(name):
            sems.append(ctx.enter_context(nc.semaphore("b_" + name)))
            return sems[-1]

        scores = ctx.enter_context(nc.psum_tensor("b_scores", [P, SLOTS, 2, 512], F32))
        out_ps = ctx.enter_context(nc.psum_tensor("b_out", [P, 512], F32))
        sum_ps = ctx.enter_context(nc.psum_tensor("b_sum", [P, 512], F32))
        k_st = [sb(f"k_st{g}", [P, HG, T], F32R) for g in range(G)]
        v_st = [sb(f"v_st{g}", [P, NK, HG * HD]) for g in range(G)]
        q_st = sb("q_st", [P, 2, HG, CW], F32R)
        prob = sb("prob", [P, RING, HG, CW])
        part = sb("part", [P, 2, HG, CW])
        res = sb("res", [P, 2, 2, CW])
        run_max = prob[:, 0]
        all_max = sb("all_max", [P, HG, CW])

        k_loaded = [[sem(f"k_loaded{g}_{n}") for n in range(PIECES)] for g in range(G)]
        v_loaded = [[sem(f"v_loaded{g}_{n}") for n in range(PIECES)] for g in range(G)]
        q_loaded = [sem(f"q_loaded{s}") for s in range(2)]
        scored, exps, pv_done, added = sem("scored"), sem("exps"), sem("pv_done"), sem("added")
        summed, sum_copied, out_copied = sem("summed"), sem("sum_copied"), sem("out_copied")
        res_stored = [sem(f"res_stored{s}") for s in range(2)]
        max_read, max_all, shifted, gate = sem("max_read"), sem("max_all"), sem("shifted"), sem("gate")

        def image_units(eng, b, unit):
            def one(g, l, i, ahead):
                u = Turn(eng, eng.snap(U * b + l + 2 * i))
                unit(g, u, l % 2, Turn(eng, eng.snap(U // 2 * b + l // 2 + i)), ahead)

            for g in range(G):
                with eng.Fori(0, NC // 2) as i:
                    for r in range(2):
                        one(g, g * NC + r, i, None)
                one(g, g * NC + NC - 1, 0, 1 - g)

        def branch(eng, fast, exact):
            ok = eng.value_load(k["bounded"][0:1, 0:1])
            with eng.If(ok > 0):
                fast()
            with eng.Else():
                exact()

        def loads(sp, pairs):
            def load_k(b, g):
                for n in range(PIECES):
                    kt0, kt1 = PIECE[n], PIECE[n + 1]
                    cols = slice(kt0 * P, min(kt1 * P, T))
                    for rep in range(2):
                        for s in range(2):
                            row = 64 * rep + 32 * s
                            sp.dma_start(k_st[g][row:row + 32, :, cols].bitcast(F32),
                                         d["k"][at(b), g, s, :, cols].rearrange("(h e) t -> e h t", e=HD)) \
                                .then_inc(k_loaded[g][n], 16)
                    sp.dma_start(v_st[g][:, kt0:kt1, :], d["v"][at(b), g, :, kt0:kt1, :]).then_inc(v_loaded[g][n], 16)

            def load_q(b, l):
                g, c = divmod(l, NC)
                for s in range(2):
                    for rep in range(2):
                        row = 64 * s + 32 * rep
                        sp.dma_start(q_st[row:row + 32, l % 2].bitcast(F32),
                                     d["q"][at(b), g, s, :, c * CW:(c + 1) * CW].rearrange("(h e) t -> e h t", e=HD)) \
                            .then_inc(q_loaded[l % 2], 16)

            def image(b, more):
                first = Turn(sp, U * b)
                sp.wait_ge(scored, START + pairs * first)
                sp.wait_ge(pv_done, START + NK * (first + 1))
                load_k(b, 1)
                for l in range(U):
                    u = first + l
                    sp.wait_ge(scored, START + pairs * u)
                    if l + 1 < U:
                        load_q(b, l + 1)
                    elif more:
                        load_q(b + 1, 0)
                    else:
                        sp.sem_inc(q_loaded[0], 64)
                    if l == NC:
                        sp.wait_ge(pv_done, START + NK * (u + 1))
                        if more:
                            load_k(b + 1, 0)
                        else:
                            sp.sem_inc(k_loaded[0][0], 64)
                    g, c = divmod(l, NC)
                    sp.wait_ge(out_copied, START + 1 * (u + 1))
                    sp.dma_start(d["att"][at(b), g, :, c * CW:(c + 1) * CW], res[:, l % 2, 0, :]) \
                        .then_inc(res_stored[l % 2], 16)
                    sp.wait_ge(sum_copied, START + 1 * (u + 1))
                    sp.dma_start(d["sums"][at(b), g, :, c * CW:(c + 1) * CW], res[0:P:HD, l % 2, 1, :]) \
                        .then_inc(res_stored[l % 2], 16)

            load_q(0, 0)
            load_k(0, 0)
            with sp.Fori(0, B - 1) as i:
                b = Turn(sp, i)
                image(b, True)
            image(B - 1, False)
            for s in range(2):
                sp.wait_ge(res_stored[s], START + 32 * (U // 2) * B)

        def score_pair(g, slot, p):
            kt, hp = divmod(p, 2)
            m = keys(kt)
            for e in range(2):
                h = 2 * hp + e
                last = nc.tensor.matmul(scores[0:m, p % SLOTS, e, 0:CW], k_st[g][:, h, kt * P:kt * P + m],
                                        q_st[:, slot, h, :], start=True, stop=True)
            last.then_inc(scored, 1)

        def weighted_values(pe, u, g, kt):
            pe.wait_ge(exps, START + NP * (u + 1) + 2 * kt + 2)
            if kt == 0:
                pe.wait_ge(out_copied, START + 1 * u)
            for h in range(HG):
                last = nc.tensor.matmul(out_ps[h * HD:(h + 1) * HD, 0:CW], v_st[g][:, kt, h * HD:(h + 1) * HD],
                                        prob[:, kt % RING, h, :], start=kt == 0, stop=kt == NK - 1)
            last.then_inc(pv_done, 1)

        def adds_until(kt, hp):
            if kt < 0:
                return adds_until(kt + NK, hp) - ADDS
            j = max(j for j in range(NG) if GROUP[j] <= kt)
            return 2 * (GROUP[j] - j + max(0, kt - GROUP[j] - 1)) + hp + 1

        def part_slot(slot, j):
            return (NG * slot + j) % 2

        def row_sums(pe, u, slot, j):
            half = part[:, part_slot(slot, j)]
            pe.wait_ge(added, START + ADDS * (u + 1) + adds_until(GROUP[j + 1] - 1, 1))
            if j == 0:
                pe.wait_ge(sum_copied, START + 1 * u)
            for h in range(HG):
                last = nc.tensor.matmul(sum_ps[h * HD:(h + 1) * HD, 0:CW], k["ones"][:], half[:, h, :],
                                        start=j == 0, stop=j == NG - 1)
            last.then_inc(summed, 1)

        def row_sums_behind(pe, u, slot, kt):
            if kt - 1 in GROUP[1:NG]:
                row_sums(pe, u, slot, GROUP.index(kt - 1) - 1)

        def add_probs(dve, u, slot, kt):
            if kt in GROUP:
                return
            j = max(j for j in range(NG) if GROUP[j] <= kt)
            rows = keys(kt)
            for hp in range(2):
                hs = slice(2 * hp, 2 * hp + 2)
                out = part[:, part_slot(slot, j), hs, :]
                dve.wait_ge(exps, START + NP * (u + 1) + 2 * kt + hp + 1)
                if kt == GROUP[j] + 1:
                    dve.wait_ge(summed, START + NG * (u + 1) + j - 1)
                    nc.vector.tensor_tensor(out, prob[:, (kt - 1) % RING, hs, :], prob[:, kt % RING, hs, :],
                                            ALU.add).then_inc(added, 1)
                else:
                    dve.wait_ge(added, START + ADDS * (u + 1) + adds_until(kt, hp) - 2)
                    nc.vector.tensor_tensor(out[0:rows], out[0:rows], prob[0:rows, kt % RING, hs, :], ALU.add) \
                        .then_inc(added, 1)

        def tile_free(eng, u, kt, hp):
            eng.wait_ge(pv_done, START + NK * (u + 1) + kt - RING + 1)
            eng.wait_ge(added, START + ADDS * (u + 1) + adds_until(kt - RING, hp))

        def copy_out(eng, copy, u, slot, use):
            eng.wait_ge(res_stored[slot], START + 32 * use)
            eng.wait_ge(pv_done, START + NK * (u + 2))
            copy(res[:, slot, 0, :], out_ps[:, 0:CW]).then_inc(out_copied, 1)

        def copy_sums(eng, copy, u, slot):
            eng.wait_ge(summed, START + NG * (u + 2))
            copy(res[:, slot, 1, :], sum_ps[:, 0:CW]).then_inc(sum_copied, 1)

        with nc.Block() as block:
            @block.sync
            def _(sp):
                for s in sems:
                    sp.sem_inc(s, START)

                branch(sp, lambda: loads(sp, NP), lambda: loads(sp, 2 * NP))

            @block.tensor
            def _(pe):
                image = []

                def fast():
                    def unit(g, u, slot, use, ahead):
                        def score(p):
                            if p == NP:
                                pe.wait_ge(q_loaded[1 - slot], START + 64 * (use + 1 + (slot == 1)))
                                if ahead is not None:
                                    k_piece(ahead, image[0] + (ahead == 0), 0)
                            if p >= NP:
                                n = p - NP
                                user = n - SLOTS if n >= SLOTS else NP - 1 - (NP - 1 - n) % SLOTS - NP
                                pe.wait_ge(exps, START + NP * (u + 2) + user + 1)
                                score_pair(g if ahead is None else ahead, 1 - slot, n)
                                return
                            if p % 2 == 0 and p // 2 in PIECE:
                                k_piece(g, image[0], PIECE.index(p // 2))
                            pe.wait_ge(exps, START + NP * (u + 1) + p - SLOTS + 1)
                            score_pair(g, slot, p)

                        for kt in range(NK):
                            values_of(g, u, slot, kt)
                            score(2 * kt + AHEAD)
                            score(2 * kt + AHEAD + 1)
                        row_sums(pe, u, slot, NG - 1)

                    def k_piece(g, b, n):
                        pe.wait_ge(k_loaded[g][n], START + 64 * (b + 1))

                    def values_of(g, u, slot, kt):
                        if kt in PIECE:
                            pe.wait_ge(v_loaded[g][PIECE.index(kt)], START + 16 * (image[0] + 1))
                        weighted_values(pe, u, g, kt)
                        row_sums_behind(pe, u, slot, kt)

                    pe.sem_inc(pv_done, NK)
                    pe.sem_inc(summed, NG)
                    pe.wait_ge(q_loaded[0], START + 64)
                    pe.wait_ge(k_loaded[0][0], START + 64)
                    for p in range(AHEAD):
                        if p >= SLOTS:
                            pe.wait_ge(exps, START + NP + p - SLOTS + 1)
                        score_pair(0, 0, p)
                    with pe.Fori(0, B) as i:
                        b = Turn(pe, i)
                        image[:] = [b]
                        image_units(pe, b, unit)

                def exact():
                    def unit(g, u, slot, use, ahead):
                        pe.wait_ge(q_loaded[slot], START + 64 * (use + 1))
                        for n in range(PIECES):
                            pe.wait_ge(k_loaded[g][n], START + 64 * (image[0] + 1))
                            pe.wait_ge(v_loaded[g][n], START + 16 * (image[0] + 1))
                        pe.wait_ge(shifted, START + NP * u)
                        for p in range(NP):
                            if p >= SLOTS:
                                pe.wait_ge(max_read, START + NP * u + p - SLOTS + 1)
                            score_pair(g, slot, p)
                        for p in range(NP):
                            if p >= SLOTS:
                                pe.wait_ge(shifted, START + NP * u + p - SLOTS + 1)
                            else:
                                pe.wait_ge(max_read, START + NP * (u + 1))
                            score_pair(g, slot, p)
                            if p % 2 and p > 2:
                                weighted_values(pe, u, g, p // 2 - 1)
                                row_sums_behind(pe, u, slot, p // 2 - 1)
                        weighted_values(pe, u, g, NK - 1)
                        row_sums(pe, u, slot, NG - 1)

                    pe.sem_inc(pv_done, NK)
                    pe.sem_inc(summed, NG)
                    with pe.Fori(0, B) as i:
                        b = Turn(pe, i)
                        image[:] = [b]
                        image_units(pe, b, unit)

                branch(pe, fast, exact)

            @block.scalar
            def _(act):
                def fast():
                    def exp(u, p):
                        kt, hp = divmod(p, 2)
                        m = keys(kt)
                        act.wait_ge(scored, START + NP * u + p + 1)
                        tile_free(act, u, kt, hp)
                        nc.scalar.activation(prob[0:m, kt % RING, 2 * hp:2 * hp + 2, :],
                                             scores[0:m, p % SLOTS, :, 0:CW], ACT.Exp, bias=-SHIFT) \
                            .then_inc(exps, 1)

                    def unit(g, u, slot, use, ahead):
                        for p in range(AHEAD, NP):
                            exp(u, p)
                        for p in range(AHEAD):
                            exp(u + 1, p)
                            if p == AHEAD - 3:
                                copy_out(act, nc.scalar.copy, u, slot, use)
                        copy_sums(act, nc.scalar.copy, u, slot)

                    act.sem_inc(exps, NP)
                    for p in range(AHEAD):
                        exp(0, p)
                    with act.Fori(0, B) as i:
                        b = Turn(act, i)
                        image_units(act, b, unit)

                def exact():
                    def unit(g, u, slot, use, ahead):
                        for p in range(NP):
                            kt, hp = divmod(p, 2)
                            m = keys(kt)
                            act.wait_ge(shifted, START + NP * u + p + 1)
                            tile = prob[0:m, kt % RING, 2 * hp:2 * hp + 2, :]
                            nc.scalar.activation(tile, tile, ACT.Exp).then_inc(exps, 1)

                    act.sem_inc(exps, NP)
                    with act.Fori(0, B) as i:
                        b = Turn(act, i)
                        image_units(act, b, unit)

                branch(act, fast, exact)

            @block.vector
            def _(dve):
                def fast():
                    def unit(g, u, slot, use, ahead):
                        for kt in range(NK):
                            add_probs(dve, u, slot, kt)

                    dve.sem_inc(added, ADDS)
                    with dve.Fori(0, B) as i:
                        b = Turn(dve, i)
                        image_units(dve, b, unit)

                def exact():
                    def unit(g, u, slot, use, ahead):
                        for p in range(NP):
                            kt, hp = divmod(p, 2)
                            m = keys(kt)
                            src = scores[0:m, p % SLOTS, :, 0:CW]
                            hs = slice(2 * hp, 2 * hp + 2)
                            dve.wait_ge(scored, START + 2 * NP * u + p + 1)
                            if kt == 0:
                                nc.vector.tensor_copy(run_max[:, hs, :], src).then_inc(max_read, 1)
                            else:
                                dve.wait_ge(max_read, START + NP * u + p - 1)
                                nc.vector.tensor_tensor(run_max[0:m, hs, :], src, run_max[0:m, hs, :], ALU.max) \
                                    .then_inc(max_read, 1)
                        dve.wait_ge(max_all, START + 1 * (u + 1))
                        for p in range(NP + 2 * 2):
                            if p < NP:
                                kt, hp = divmod(p, 2)
                                m = keys(kt)
                                hs = slice(2 * hp, 2 * hp + 2)
                                dve.wait_ge(scored, START + 2 * NP * u + NP + p + 1)
                                tile_free(dve, u, kt, hp)
                                nc.vector.tensor_tensor(prob[0:m, kt % RING, hs, :], scores[0:m, p % SLOTS, :, 0:CW],
                                                        all_max[0:m, hs, :], ALU.subtract).then_inc(shifted, 1)
                            if p >= 4 and p % 2:
                                add_probs(dve, u, slot, (p - 4) // 2)
                        copy_out(dve, nc.vector.tensor_copy, u, slot, use)
                        copy_sums(dve, nc.vector.tensor_copy, u, slot)

                    dve.sem_inc(added, ADDS)
                    with dve.Fori(0, B) as i:
                        b = Turn(dve, i)
                        image_units(dve, b, unit)

                branch(dve, fast, exact)

            @block.gpsimd
            def _(pool):
                def exact():
                    with pool.Fori(0, B * U) as i:
                        u = Turn(pool, i)
                        pool.wait_ge(max_read, START + NP * (u + 1))
                        pool.wait_ge(shifted, START + NP * u)
                        pool.sem_inc(gate, 1)
                        nc.gpsimd.partition_all_reduce(all_max[:].rearrange("p h t -> p (h t)"),
                                                       run_max.rearrange("p h t -> p (h t)"), P,
                                                       bass.bass_isa.ReduceOp.max).then_inc(max_all, 1)

                ok = pool.value_load(k["bounded"][0:1, 0:1])
                with pool.If(ok < 1):
                    exact()


def part_c(nc, k, B, d, w_proj, Wf, bf, Wg, bg, Wh, bh, out):
    with ExitStack() as ctx:
        def sb(name, shape, dt=F32):
            return ctx.enter_context(nc.sbuf_tensor("c_" + name, shape, dt))

        sems = []

        def sem(name):
            sems.append(ctx.enter_context(nc.semaphore("c_" + name)))
            return sems[-1]

        bank = [ctx.enter_context(nc.psum_tensor(f"c_bank{i}", [P, 512], F32)) for i in range(8)]
        bank_p, bank_fg, bank_s, bank_h, bank_o = bank[0:2], bank[2], bank[3], bank[4:6], bank[6:8]
        CK = Wf.shape[1]
        att = sb("att", [P, G, T])
        inv = sb("inv", [P, G, T])
        flat = sb("flat", [P, B, G * HG * T // P])
        yT = sb("yT", [P, CH, T])
        yn = sb("yn", [P, CH, T])
        y_nat = sb("y_nat", [TW, NT, C])
        fg = sb("fg", [CK, 2, 2, CW])
        sig = sb("sig", [TW, 2, TPC, TW])
        weights = sb("weights", [TW, 2, TPC, TW])
        h_sb = sb("h_sb", [TW, 2, TPC, C])
        z = sb("z", [TW, 2, TPC, C])
        wp = sb("wp", [P, CH, C])
        wfg = sb("wfg", [P, CH, 2 * CK])
        wh = sb("wh", [P, CH, C])
        bias_fg = sb("bias_fg", [2 * CK, 1])
        bias_h = sb("bias_h", [TW, 2, C])

        w_loaded = sem("w_loaded")
        x_loaded = [sem(f"x_loaded{c}") for c in range(NC)]
        att_loaded = [sem(f"att_loaded{c}") for c in range(NC)]
        sums_loaded = [sem(f"sums_loaded{b}") for b in range(B)]
        inv_done, att_done = sem("inv_done"), sem("att_done")
        inv_stored = [sem(f"inv_stored{b}") for b in range(B)]
        p_done, y_done, normed = sem("p_done"), sem("y_done"), sem("normed")
        tr_done, tr_read = sem("tr_done"), sem("tr_read")
        fg_done, fg_read, s_done, sig_done, masked = (sem("fg_done"), sem("fg_read"), sem("s_done"),
                                                      sem("sig_done"), sem("masked"))
        h_done, h_read, o_done, z_done = sem("h_done"), sem("h_read"), sem("o_done"), sem("z_done")
        z_stored = [sem(f"z_stored{s}") for s in range(2)]
        gn = GroupNorm(nc, sb, sem, k, bank_p[0])
        NP2 = NT // 2
        out_tok = out.rearrange("b h w c -> b (h w) c").rearrange("b (t p) c -> b p t c", p=TW)
        AHEAD = 3

        def slot_users(c):
            return max(0, c - 1)

        with nc.Block() as block:
            @block.sync
            def _(sp):
                for s in sems:
                    sp.sem_inc(s, START)

                def load(b):
                    for c in range(NC):
                        s = slice(c * CW, (c + 1) * CW)
                        sp.dma_start(att[:, :, s], d["att"][at(b), :, :, s].rearrange("g p t -> p g t")) \
                            .then_inc(att_loaded[c], 16)
                        for h in range(HG):
                            src = d["inv"][at(b), :, h:h + 1, s].rearrange("g a t -> a g t")
                            sp.dma_start(inv[h * HD:(h + 1) * HD, :, s], src.broadcast_to([HD, G, CW])) \
                                .then_inc(att_loaded[c], 16)
                        sp.dma_start(yT[:, :, s], d["xT"][at(b), :, :, s].rearrange("h p t -> p h t")) \
                            .then_inc(x_loaded[c], 16)

                def store(b, c):
                    sp.wait_ge(z_done, START + NP2 * b + 2 * (c + 1))
                    sp.dma_start(out_tok[at(b), :, c * TPC:(c + 1) * TPC, :], z[:, c % 2]).then_inc(z_stored[c % 2], 16)

                def image(b, more):
                    if more:
                        sp.wait_ge(p_done, START + NP2 * (b + 1))
                        sp.wait_ge(normed, START + NP2 * (b + 1))
                        sp.wait_ge(tr_done, START + NP2 * (b + 1))
                        load(b + 1)
                    for c in range(NC):
                        store(b, c)

                sp.dma_start(wp[:], w_proj.rearrange("(h p) n -> p h n", p=P)).then_inc(w_loaded, 16)
                sp.dma_start(wfg[:, :, 0:CK], Wf.rearrange("(h p) n -> p h n", p=P)).then_inc(w_loaded, 16)
                sp.dma_start(wfg[:, :, CK:], Wg.rearrange("(h p) n -> p h n", p=P)).then_inc(w_loaded, 16)
                sp.dma_start(wh[:], Wh.rearrange("(h p) n -> p h n", p=P)).then_inc(w_loaded, 16)
                sp.dma_start(bias_fg[0:CK], bf.rearrange("(p a) -> p a", a=1)).then_inc(w_loaded, 16)
                sp.dma_start(bias_fg[CK:], bg.rearrange("(p a) -> p a", a=1)).then_inc(w_loaded, 16)
                for e in range(2):
                    sp.dma_start(bias_h[:, e, :], bh.rearrange("(a n) -> a n", a=1).broadcast_to([TW, C])) \
                        .then_inc(w_loaded, 16)
                spread = lambda t: t.rearrange("g h t -> (g h t)").rearrange("(p n) -> p n", p=P)
                for b in range(B):
                    sp.dma_start(flat[:, b, :], spread(d["sums"][b])).then_inc(sums_loaded[b], 16)
                for b in range(B):
                    sp.wait_ge(inv_done, START + b + 1)
                    sp.dma_start(spread(d["inv"][b]), flat[:, b, :]).then_inc(inv_stored[b], 16)
                for b in range(B):
                    sp.wait_ge(inv_stored[b], START + 16)
                load(0)
                with sp.Fori(0, B - 1) as i:
                    b = Turn(sp, i)
                    image(b, True)
                image(B - 1, False)
                sp.wait_ge(z_stored[0], START + 16 * ((NC + 1) // 2) * B)
                sp.wait_ge(z_stored[1], START + 16 * (NC // 2) * B)

            @block.tensor
            def _(pe):
                def project(b):
                    for i in range(CH * NC):
                        c, ch = divmod(i, CH)
                        if ch == 0:
                            pe.wait_ge(att_done, START + G * (NC * b + c + 1))
                        pe.wait_ge(y_done, START + NP2 * b + max(0, i - 1))
                        for g in range(G):
                            last = nc.tensor.matmul(bank_p[ch][:, 0:CW], wp[:, g, ch * P:(ch + 1) * P],
                                                    att[:, g, c * CW:(c + 1) * CW], start=g == 0, stop=g == G - 1)
                        last.then_inc(p_done, 1)

                def average_means(b):
                    pe.wait_ge(y_done, START + NP2 * (b + 1))
                    gn.average_means(pe, b)

                def transposes(b):
                    pe.wait_ge(y_done, START + NP2 * (b + 1))
                    for i in range(NP2):
                        if i < 2:
                            pe.wait_ge(z_done, START + NP2 * b)
                        else:
                            pe.wait_ge(tr_read, START + NP2 * b + i - 1)
                        for e in range(2):
                            for ch in range(CH):
                                t = 2 * i + e
                                last = nc.tensor.transpose(bank_o[i % 2][0:TW, e * C + ch * P:e * C + (ch + 1) * P],
                                                           yT[:, ch, t * TW:(t + 1) * TW], k["ident"][:])
                        last.then_inc(tr_done, 1)

                def f_g_h_scores(b, c):
                    pe.wait_ge(normed, START + CH * (NC * b + c + 1))
                    pe.wait_ge(fg_read, START + 2 * (NC * b + c))
                    for ch in range(CH):
                        last = nc.tensor.matmul(bank_fg[0:2 * CK, 0:CW], wfg[:, ch, :], yn[:, ch, c * CW:(c + 1) * CW],
                                                start=ch == 0, stop=ch == CH - 1)
                    last.then_inc(fg_done, 1)
                    for e in range(2):
                        pe.wait_ge(h_read, START + NP2 * b + max(0, 2 * c + e - 1))
                        for t in range(2):
                            first = (c * TPC + 2 * e + t) * TW
                            for ch in range(CH):
                                last = nc.tensor.matmul(bank_h[e][0:TW, t * C:(t + 1) * C], yn[:, ch, first:first + TW],
                                                        wh[:, ch, :], start=ch == 0, stop=ch == CH - 1)
                        last.then_inc(h_done, 1)
                    pe.wait_ge(fg_read, START + 2 * (NC * b + c + 1))
                    pe.wait_ge(sig_done, START + NC * b + c)
                    for t in range(TPC):
                        ts = slice(t * TW, (t + 1) * TW)
                        last = nc.tensor.matmul(bank_s[0:TW, ts], fg[:, c % 2, 1, ts], fg[:, c % 2, 0, ts],
                                                start=True, stop=True)
                    last.then_inc(s_done, 1)

                def weighted_h(b, c):
                    pe.wait_ge(masked, START + NC * b + c + 1)
                    pe.wait_ge(h_read, START + NP2 * b + 2 * (c + 1))
                    for e in range(2):
                        i = 2 * c + e
                        if i < 2:
                            pe.wait_ge(tr_read, START + NP2 * (b + 1))
                        else:
                            pe.wait_ge(z_done, START + NP2 * b + i - 1)
                        for t in range(2):
                            last = nc.tensor.matmul(bank_o[e][0:TW, t * C:(t + 1) * C],
                                                    weights[:, c % 2, 2 * e + t, :], h_sb[:, c % 2, 2 * e + t, :],
                                                    start=True, stop=True)
                        last.then_inc(o_done, 1)

                def image(b, more):
                    transposes(b)
                    for c in range(NC):
                        f_g_h_scores(b, c)
                        if c:
                            weighted_h(b, c - 1)
                        if more and c == AHEAD:
                            project(b + 1)
                        if more and c == AHEAD + 1:
                            average_means(b + 1)
                        if more and c == AHEAD + 2:
                            gn.average_spread(pe, b + 1)
                    weighted_h(b, NC - 1)

                pe.wait_ge(w_loaded, START + 16 * 8)
                project(0)
                average_means(0)
                gn.average_spread(pe, 0)
                with pe.Fori(0, B - 1) as i:
                    b = Turn(pe, i)
                    image(b, True)
                image(B - 1, False)

            @block.scalar
            def _(act):
                def image(b):
                    act.wait_ge(z_done, START + NP2 * b)
                    for i in range(NP2):
                        act.wait_ge(tr_done, START + NP2 * b + i + 1)
                        nc.scalar.copy(y_nat[:, 2 * i:2 * i + 2, :],
                                       bank_o[i % 2][0:TW, :].rearrange("p (t c) -> p t c", c=C)).then_inc(tr_read, 1)
                    for c in range(NC):
                        act.wait_ge(fg_done, START + NC * b + c + 1)
                        act.wait_ge(s_done, START + NC * b + slot_users(c))
                        for n in range(2):
                            nc.scalar.activation(fg[:, c % 2, n, :], bank_fg[n * CK:(n + 1) * CK, 0:CW], ACT.Identity,
                                                 bias=bias_fg[n * CK:(n + 1) * CK, :]).then_inc(fg_read, 1)
                        act.wait_ge(s_done, START + NC * b + c + 1)
                        act.wait_ge(masked, START + NC * b + slot_users(c))
                        nc.scalar.activation(sig[:, c % 2].rearrange("p t n -> p (t n)"), bank_s[0:TW, 0:CW],
                                             ACT.Sigmoid).then_inc(sig_done, 1)

                act.wait_ge(w_loaded, START + 16 * 8)
                with act.Fori(0, B) as i:
                    b = Turn(act, i)
                    image(b)

            @block.gpsimd
            def _(pool):
                def image(b, more):
                    for c in range(NC):
                        pool.wait_ge(sig_done, START + NC * b + c + 1)
                        pool.wait_ge(o_done, START + NP2 * b + 2 * slot_users(c))
                        nc.gpsimd.tensor_tensor(weights[:, c % 2], sig[:, c % 2],
                                                k["row_mask"][0:TW, None, :].broadcast_to([TW, TPC, TW]),
                                                ALU.mult).then_inc(masked, 1)
                        if more and c <= AHEAD:
                            for n in range(NC * c // (AHEAD + 1), NC * (c + 1) // (AHEAD + 1)):
                                divide(b + 1, n)
                        if more and c == AHEAD + 2:
                            gn.rstd(pool, b + 1)

                def divide(b, c):
                    pool.wait_ge(att_loaded[c], START + 80 * (b + 1))
                    for g in range(G):
                        s = att[:, g, c * CW:(c + 1) * CW]
                        nc.gpsimd.tensor_tensor(s, s, inv[:, g, c * CW:(c + 1) * CW], ALU.mult).then_inc(att_done, 1)

                for c in range(NC):
                    divide(0, c)
                gn.rstd(pool, 0)
                with pool.Fori(0, B - 1) as i:
                    b = Turn(pool, i)
                    image(b, True)
                image(B - 1, False)

            @block.vector
            def _(dve):
                v = nc.vector

                def add_residual(b):
                    for i in range(CH * NC):
                        c, ch = divmod(i, CH)
                        if ch == 0:
                            dve.wait_ge(x_loaded[c], START + 16 * (b + 1))
                        s = yT[:, ch, c * CW:(c + 1) * CW]
                        dve.wait_ge(p_done, START + NP2 * b + i + 1)
                        v.tensor_tensor(s, bank_p[ch][:, 0:CW], s, ALU.add).then_inc(y_done, 1)
                        if i:
                            dve.wait_ge(y_done, START + NP2 * b + i)
                            gn.stats(yT, *divmod(i - 1, CH))
                    dve.wait_ge(y_done, START + NP2 * (b + 1))
                    gn.stats(yT, NC - 1, CH - 1)
                    gn.aggregate(dve, b)

                def norm(b):
                    dve.wait_ge(gn.rstd_done, START + 1 * (b + 1))
                    dve.wait_ge(h_done, START + NP2 * b)
                    for c in range(NC):
                        for ch in range(CH):
                            gn.norm(yn, yT, c, ch).then_inc(normed, 1)

                def h_rows(b, c):
                    dve.wait_ge(o_done, START + NP2 * b + 2 * slot_users(c))
                    for e in range(2):
                        dve.wait_ge(h_done, START + NP2 * b + 2 * c + e + 1)
                        v.tensor_tensor(h_sb[:, c % 2, 2 * e:2 * e + 2, :],
                                        bank_h[e][0:TW, :].rearrange("p (t c) -> p t c", c=C), bias_h[:], ALU.add) \
                            .then_inc(h_read, 1)

                def results(b, c):
                    users = (NC + 1) // 2 if c % 2 == 0 else NC // 2
                    dve.wait_ge(z_stored[c % 2], START + 16 * (users * b + c // 2))
                    for e in range(2):
                        t = TPC * c + 2 * e
                        dve.wait_ge(o_done, START + NP2 * b + 2 * c + e + 1)
                        v.tensor_tensor(z[:, c % 2, 2 * e:2 * e + 2, :],
                                        bank_o[e][0:TW, :].rearrange("p (t c) -> p t c", c=C),
                                        y_nat[:, t:t + 2, :], ALU.add).then_inc(z_done, 1)

                def image(b, more):
                    norm(b)
                    dve.wait_ge(tr_read, START + NP2 * (b + 1))
                    for c in range(NC):
                        h_rows(b, c)
                        if c:
                            results(b, c - 1)
                        if more and c == AHEAD:
                            add_residual(b + 1)
                        if more and c == AHEAD + 1:
                            gn.spread(dve, b + 1)
                        if more and c == AHEAD + 2:
                            gn.variance(dve, b + 1)
                    results(b, NC - 1)

                for b in range(B):
                    dve.wait_ge(sums_loaded[b], START + 16)
                    v.reciprocal(flat[:, b, :], flat[:, b, :]).then_inc(inv_done, 1)
                dve.wait_ge(w_loaded, START + 16 * 8)
                add_residual(0)
                gn.spread(dve, 0)
                gn.variance(dve, 0)
                with dve.Fori(0, B - 1) as i:
                    b = Turn(dve, i)
                    image(b, True)
                image(B - 1, False)


def build(nc, x, w_qkv, w_proj, Wf, bf, Wg, bg, Wh, bh, out):
    B = x.shape[0]
    nc.disable_value_cache = True
    d = dict(
        xT=nc.dram_tensor("xT_scratch", (B, CH, P, T), F32).ap(),
        q=nc.dram_tensor("q_scratch", (B, G, 2, P, T), F32).ap(),
        k=nc.dram_tensor("k_scratch", (B, G, 2, P, T), F32).ap(),
        v=nc.dram_tensor("v_scratch", (B, G, P, NK, P), F32).ap(),
        att=nc.dram_tensor("att_scratch", (B, G, P, T), F32).ap(),
        sums=nc.dram_tensor("sums_scratch", (B, G, HG, T), F32).ap(),
        inv=nc.dram_tensor("inv_scratch", (B, G, HG, T), F32).ap(),
    )
    with ExitStack() as ctx:
        k = build_consts(nc, ctx)
        part_a(nc, k, B, x, w_qkv, d)
        part_b(nc, k, B, d)
        part_c(nc, k, B, d, w_proj, Wf, bf, Wg, bg, Wh, bh, out)


_INS = ["x", "L0_conv_w_qkv", "L0_conv_w_proj", "L1_conv_Wf", "L1_conv_bf", "L1_conv_Wg", "L1_conv_bg",
        "L1_conv_Wh", "L1_conv_bh"]


def kernel(**inputs):
    import numpy as _np
    import concourse.bacc as _bacc
    from concourse import mybir as _mybir
    from concourse.bass_utils import run_bass_kernel_spmd as _run

    nc = _bacc.Bacc("TRN2", target_bir_lowering=False, num_devices=1)
    arrays, args = {}, []
    for name in _INS:
        a = _np.ascontiguousarray(inputs[name])
        arrays[f"in_{name}"] = a
        args.append(nc.dram_tensor(f"in_{name}", a.shape, _mybir.dt.from_np(a.dtype), kind="ExternalInput").ap())
    out = nc.dram_tensor("out_y", inputs["x"].shape, _mybir.dt.float32, kind="ExternalOutput").ap()
    build(nc, *args, out)
    return _run(nc, [arrays], core_ids=[0]).results[0]["out_y"]
```

```python
from contextlib import ExitStack

import concourse.bass as bass
from concourse import mybir

F32 = mybir.dt.float32
F32R = mybir.dt.float32r
BF16 = mybir.dt.bfloat16
I32 = mybir.dt.int32
ACT = mybir.ActivationFunctionType
ALU = mybir.AluOpType
AX = mybir.AxisListType

P = 128
C = 256
CH = C // P
SIDE = 56
T = SIDE * SIDE
HD = 32
HG = 4
G = 2
CW = 448
NC = T // CW
TW = 2 * SIDE
TPC = CW // TW
NT = T // TW
NK = (T + P - 1) // P
KLAST = T - (NK - 1) * P
GSIZE = C // 32
EPS = 1e-5
SCALE = float(HD) ** -0.25

SHIFT = 40.0
SCORE_BOUND = 100.0
MEAN_BOUND = 10.0
WV_BOUND = 1e3
SLACK = 1.02


def keys(kt):
    return KLAST if kt == NK - 1 else P


def build_consts(nc, ctx):
    def sb(name, shape, dt=F32):
        return ctx.enter_context(nc.sbuf_tensor(name, shape, dt))

    k = dict(
        ident=sb("ident", [P, P]),
        group_avg=sb("group_avg", [P, P]),
        head_sum=sb("head_sum", [P, P]),
        head_sum_bf=sb("head_sum_bf", [P, P], BF16),
        ones=sb("ones", [P, HD]),
        minus_half=sb("minus_half", [P, CH]),
        row_mask=sb("row_mask", [TW, TW]),
        norm_max=sb("norm_max", [P, 4, 4]),
        xn_mean=sb("xn_mean", [P, CH, 4]),
        bounded=sb("bounded", [P, 1], I32),
    )
    made = ctx.enter_context(nc.semaphore("consts_made"))
    count = [0]
    with nc.Block() as block:
        @block.gpsimd
        def _(pool):
            def step(ins):
                ins.then_inc(made, 1)
                count[0] += 1
                pool.wait_ge(made, count[0])

            def blocks(t, value, width):
                n = t.shape[1] // width
                v = t[:].rearrange("p (n w) -> p n w", w=width)
                step(nc.gpsimd.memset(t[:], value))
                step(nc.gpsimd.affine_select(out=v, in_=v, compare_op=ALU.is_ge, fill=0.0, base=0,
                                             pattern=[[-width, n], [0, width]], channel_multiplier=1))
                step(nc.gpsimd.affine_select(out=v, in_=v, compare_op=ALU.is_ge, fill=0.0, base=width - 1,
                                             pattern=[[width, n], [0, width]], channel_multiplier=-1))

            step(nc.gpsimd.memset(k["ident"][:], 0.0))
            step(nc.gpsimd.affine_select(out=k["ident"][:], in_=k["ident"][:], compare_op=ALU.not_equal, fill=1.0,
                                         base=0, pattern=[[-1, P]], channel_multiplier=1))
            blocks(k["group_avg"], 1.0 / GSIZE, GSIZE)
            blocks(k["head_sum"], 1.0, HD)
            blocks(k["row_mask"], 1.0, SIDE)
            step(nc.gpsimd.tensor_copy(k["head_sum_bf"][:], k["head_sum"][:]))
            step(nc.gpsimd.memset(k["ones"][:], 1.0))
            step(nc.gpsimd.memset(k["minus_half"][:], -0.5))
    return k


START = 1


class Turn:

    def __init__(self, eng, value, offset=0, kept=None):
        self.eng, self.value, self.offset = eng, value, offset
        self.kept = {} if kept is None else kept

    def __mul__(self, n):
        if isinstance(self.value, int):
            return (self.value + self.offset) * n
        if n not in self.kept:
            self.kept[n] = self.eng.snap(self.value * n)
        return self.kept[n] + self.offset * n

    __rmul__ = __mul__

    def __add__(self, n):
        return Turn(self.eng, self.value, self.offset + n, self.kept)


def at(turn):
    return turn.value + turn.offset if isinstance(turn, Turn) else turn


class GroupNorm:

    def __init__(self, nc, sb, sem, k, psum):
        self.nc, self.k, self.psum = nc, k, psum
        self.chunk_stats = sb("chunk_stats", [P, CH, NC, 6])
        self.moments = sb("moments", [P, CH, 2])
        self.off = sb("off", [P, CH])
        self.spread_t = sb("spread", [P, CH])
        self.mean = sb("mean", [P, CH])
        self.var = sb("var", [P, CH])
        self.rstd_t = sb("rstd", [P, CH])
        self.stat_done = sem("stat_done")
        self.aggregated = sem("aggregated")
        self.means_avg = sem("means_avg")
        self.spread_done = sem("spread_done")
        self.spread_avg = sem("spread_avg")
        self.var_done = sem("var_done")
        self.rstd_done = sem("rstd_done")
        self.gate = sem("gate")

    def stats(self, src, c, ch):
        self.nc.vector.bn_stats(self.chunk_stats[:, ch, c, :],
                                src[:, ch, c * CW:(c + 1) * CW]).then_inc(self.stat_done, 1)

    def aggregate(self, dve, b):
        dve.wait_ge(self.stat_done, START + CH * NC * (b + 1))
        dve.sem_inc(self.gate, 1)
        for ch in range(CH):
            self.nc.vector.bn_aggr(self.moments[:, ch, :], self.chunk_stats[:, ch, :, :]) \
                .then_inc(self.aggregated, 1)

    def average_means(self, pe, b):
        pe.wait_ge(self.aggregated, START + CH * (b + 1))
        self.nc.tensor.matmul(self.psum[:, 0:CH], self.k["group_avg"][:], self.moments[:, :, 0],
                              start=True, stop=True).then_inc(self.means_avg, 1)

    def spread(self, dve, b):
        v = self.nc.vector
        dve.wait_ge(self.means_avg, START + 1 * (b + 1))
        v.tensor_copy(self.mean[:], self.psum[:, 0:CH]).then_inc(self.spread_done, 1)
        dve.wait_ge(self.spread_done, START + 3 * b + 1)
        v.tensor_tensor(self.off[:], self.moments[:, :, 0], self.mean[:], ALU.subtract) \
            .then_inc(self.spread_done, 1)
        dve.wait_ge(self.spread_done, START + 3 * b + 2)
        v.tensor_tensor(self.spread_t[:], self.off[:], self.off[:], ALU.mult).then_inc(self.spread_done, 1)
        dve.wait_ge(self.spread_done, START + 3 * b + 3)
        v.tensor_tensor(self.var[:], self.spread_t[:], self.moments[:, :, 1], ALU.add) \
            .then_inc(self.var_done, 1)

    def average_spread(self, pe, b):
        pe.wait_ge(self.var_done, START + 2 * b + 1)
        self.nc.tensor.matmul(self.psum[:, CH:2 * CH], self.k["group_avg"][:], self.var[:],
                              start=True, stop=True).then_inc(self.spread_avg, 1)

    def variance(self, dve, b):
        dve.wait_ge(self.spread_avg, START + 1 * (b + 1))
        self.nc.vector.tensor_scalar(self.spread_t[:], self.psum[:, CH:2 * CH], EPS, None, ALU.add) \
            .then_inc(self.var_done, 1)

    def rstd(self, pool, b):
        pool.wait_ge(self.var_done, START + 2 * b + 2)
        self.nc.gpsimd.tensor_tensor(self.rstd_t[:], self.spread_t[:], self.k["minus_half"][:], ALU.pow) \
            .then_inc(self.rstd_done, 1)

    def norm(self, dst, src, c, ch):
        s = slice(c * CW, (c + 1) * CW)
        return self.nc.vector.tensor_scalar(dst, src[:, ch, s], self.mean[:, ch:ch + 1],
                                            self.rstd_t[:, ch:ch + 1], ALU.subtract, ALU.mult)


def three_passes(nc, out, left, right, first=True, last=True):
    (lh, ll), (rh, rl) = left, right
    nc.tensor.matmul(out, lh, rh, start=first, stop=False)
    nc.tensor.matmul(out, lh, rl, start=False, stop=False)
    return nc.tensor.matmul(out, ll, rh, start=False, stop=last)


def part_a(nc, k, B, x, w_qkv, d):
    PR = 2 * NC
    SR = 4
    XR = 2
    NQ = 4 * NC
    with ExitStack() as ctx:
        def sb(name, shape, dt=F32):
            return ctx.enter_context(nc.sbuf_tensor("a_" + name, shape, dt))

        sems = []

        def sem(name):
            sems.append(ctx.enter_context(nc.semaphore("a_" + name)))
            return sems[-1]

        bank = [ctx.enter_context(nc.psum_tensor(f"a_bank{i}", [P, 512], F32)) for i in range(8)]
        bank_t, bank_q, bank_n, bank_v = bank[0:2], bank[2:5], bank[5], bank[6:8]
        x_in = sb("x_in", [TW, NT, C])
        xT = sb("xT", [P, CH, T])
        xn = sb("xn", [P, XR, CH, CW])
        xn_high = sb("xn_high", [P, CH, T], F32R)
        xn_low = sb("xn_low", [P, CH, T], F32R)
        w = sb("w", [P, CH, 3 * C])
        w_high = sb("w_high", [P, CH, 3 * C], F32R)
        w_low = sb("w_low", [P, CH, 3 * C], F32R)
        parts = sb("parts", [P, PR, 2, CW], F32R)
        square = sb("square", [P, SR, CW], BF16)
        v_st = sb("v_st", [P, G, NK, HG * HD])
        item_max = sb("item_max", [P, NQ])
        kmean2 = sb("kmean2", [P, G * B])
        bound = sb("bound", [P, 2 * G * B + 1])
        worst = sb("worst", [P, 2])

        w_loaded, x_stored, v_stored = sem("w_loaded"), sem("x_stored"), sem("v_stored")
        x_loaded = [sem(f"x_loaded{c}") for c in range(NC)]
        part_stored = [sem(f"part_stored{n}") for n in range(PR)]
        t_done, t_act, t_dve = sem("t_done"), sem("t_act"), sem("t_dve")
        normed = sem("normed")
        w_split, x_high, x_low = sem("w_split"), sem("x_high"), sem("x_low")
        q_done, q_high, q_low = sem("q_done"), sem("q_high"), sem("q_low")
        squared, summed, max_taken = sem("squared"), sem("summed"), sem("max_taken")
        v_done, v_act, v_dve, v_zero = sem("v_done"), sem("v_act"), sem("v_dve"), sem("v_zero")
        end_pe, end_dve, end_pool, image_max = sem("end_pe"), sem("end_dve"), sem("end_pool"), sem("image_max")
        mean_saved = sem("mean_saved")
        gn = GroupNorm(nc, sb, sem, k, bank_n)
        x_tok = x.rearrange("b h w c -> b (h w) c").rearrange("b (t p) c -> b p t c", p=TW)
        VA, VD = (NK + 1) // 2, NK // 2
        V_PIECE = [0, 10, 20, NK]
        VS = 16 * (len(V_PIECE) - 1)
        CHUNK_AFTER = {2 * c + 1: c for c in range(NC)}
        MEANS, SPREAD_PE, SPREAD_DVE, VARIANCE, NORM0 = 16, 19, 17, 19, 21

        with nc.Block() as block:
            @block.sync
            def _(sp):
                for s in sems:
                    sp.sem_inc(s, START)

                def load_x(b, c):
                    sp.dma_start(x_in[:, c * TPC:(c + 1) * TPC, :], x_tok[at(b), :, c * TPC:(c + 1) * TPC, :]) \
                        .then_inc(x_loaded[c], 16)

                def image(b, more):
                    sp.wait_ge(t_act, START + NC * (b + 1))
                    sp.wait_ge(t_dve, START + NC * (b + 1))
                    sp.dma_start(d["xT"][at(b)].rearrange("h p t -> p h t"), xT[:]).then_inc(x_stored, 16)
                    if more:
                        for c in range(NC):
                            load_x(b + 1, c)
                    for c in range(NC):
                        for j in range(4):
                            dst = d["q" if j < 2 else "k"][at(b), j % 2]
                            n = (4 * c + j) % PR
                            sp.wait_ge(q_low, START + NQ * b + 4 * c + j + 1)
                            sp.dma_start(dst[:, :, c * CW:(c + 1) * CW].rearrange("s p t -> p s t"),
                                         parts[:, n].bitcast(F32)).then_inc(part_stored[n], 16)
                    for k0, k1 in zip(V_PIECE, V_PIECE[1:]):
                        sp.wait_ge(v_act, START + VA * b + (k1 + 1) // 2)
                        sp.wait_ge(v_dve, START + VD * b + k1 // 2)
                        sp.dma_start(d["v"][at(b), :, :, k0:k1, :].rearrange("g p k n -> p g k n"),
                                     v_st[:, :, k0:k1, :]).then_inc(v_stored, 16)

                for c in range(NC):
                    load_x(0, c)
                    if c == 0:
                        sp.dma_start(w[:], w_qkv.rearrange("(h p) n -> p h n", p=P)).then_inc(w_loaded, 16)
                with sp.Fori(0, B - 1) as i:
                    b = Turn(sp, i)
                    image(b, True)
                image(B - 1, False)
                sp.wait_ge(x_stored, START + 16 * B)
                sp.wait_ge(v_stored, START + VS * B)
                for n in range(PR):
                    sp.wait_ge(part_stored[n], START + 16 * (NQ // PR) * B)

            @block.tensor
            def _(pe):
                def transposes(b, c):
                    pe.wait_ge(x_loaded[c], START + 16 * (b + 1))
                    for ch, freed in ((0, t_act), (1, t_dve)):
                        if not (isinstance(b, int) and b == 0 and c == 0):
                            pe.wait_ge(freed, START + NC * b + c)
                        for t in range(TPC):
                            last = nc.tensor.transpose(bank_t[ch][:, t * TW:(t + 1) * TW],
                                                       x_in[:, c * TPC + t, ch * P:(ch + 1) * P],
                                                       k["ident"][0:TW, 0:TW])
                        last.then_inc(t_done, 1)

                def head_norms(b, i):
                    pe.wait_ge(squared, START + NQ * b + i + 1)
                    pe.wait_ge(max_taken, START + NQ * b + i)
                    nc.tensor.matmul(bank_n[:, 0:CW], k["head_sum_bf"][:], square[:, i % SR, :],
                                     start=True, stop=True).then_inc(summed, 1)

                def q_and_k(b):
                    for i in range(NQ):
                        c, j = divmod(i, 4)
                        if j == 0:
                            pe.wait_ge(x_low, START + NC * b + c + 1)
                        pe.wait_ge(q_low, START + NQ * b + max(0, i - 2))
                        ws, xs = slice(j * P, (j + 1) * P), slice(c * CW, (c + 1) * CW)
                        for ch in range(CH):
                            last = three_passes(nc, bank_q[i % 3][:, 0:CW], (w_high[:, ch, ws], w_low[:, ch, ws]),
                                                (xn_high[:, ch, xs], xn_low[:, ch, xs]), ch == 0, ch == CH - 1)
                        last.then_inc(q_done, 1)
                        if i >= 3:
                            head_norms(b, i - 3)

                def values(b, more):
                    for kt in range(NK):
                        if kt < 3:
                            head_norms(b, NQ - 3 + kt)
                        freed, n = (v_dve, VD) if kt % 2 else (v_act, VA)
                        pe.wait_ge(freed, START + n * b + kt // 2)
                        m = keys(kt)
                        xs, ws = slice(kt * P, kt * P + m), slice(2 * C, 3 * C)
                        for ch in range(CH):
                            last = three_passes(nc, bank_v[kt % 2][0:m, 0:C], (xn_high[:, ch, xs], xn_low[:, ch, xs]),
                                                (w_high[:, ch, ws], w_low[:, ch, ws]), ch == 0, ch == CH - 1)
                        last.then_inc(v_done, 1)
                        if more and kt in CHUNK_AFTER:
                            transposes(b + 1, CHUNK_AFTER[kt])
                        if more and kt == MEANS:
                            pe.wait_ge(max_taken, START + NQ * (b + 1))
                            gn.average_means(pe, b + 1)
                        if more and kt == SPREAD_PE:
                            gn.average_spread(pe, b + 1)

                for c in range(NC):
                    transposes(0, c)
                gn.average_means(pe, 0)
                gn.average_spread(pe, 0)
                pe.wait_ge(w_split, START + 2)
                with pe.Fori(0, B - 1) as i:
                    b = Turn(pe, i)
                    q_and_k(b)
                    values(b, True)
                q_and_k(B - 1)
                values(B - 1, False)
                pe.wait_ge(mean_saved, START + B)
                pe.wait_ge(max_taken, START + NQ * B)
                for g in range(G):
                    for ch in range(CH):
                        last = nc.tensor.matmul(bank_n[:, g * B:(g + 1) * B],
                                                w[:, ch, C + g * P:C + (g + 1) * P], k["xn_mean"][:, ch, 0:B],
                                                start=ch == 0, stop=ch == CH - 1)
                last.then_inc(end_pe, 1)
                pe.wait_ge(end_dve, START + 2)
                nc.tensor.matmul(bank_q[0][:, 0:G * B], k["head_sum"][:], kmean2[:], start=True, stop=True) \
                    .then_inc(end_pe, 1)

            @block.scalar
            def _(act):
                def evacuate_x(b, c):
                    if c == 0 and not isinstance(b, int):
                        act.wait_ge(normed, START + CH * NC * b)
                        act.wait_ge(x_stored, START + 16 * b)
                    act.wait_ge(t_done, START + CH * (NC * b + c) + 1)
                    nc.scalar.copy(xT[:, 0, c * CW:(c + 1) * CW], bank_t[0][:, 0:CW]).then_inc(t_act, 1)

                def split_x(b, c):
                    act.wait_ge(normed, START + CH * (NC * b + c + 1))
                    if c:
                        act.wait_ge(v_done, START + NK * b)
                    elif not isinstance(b, int):
                        act.wait_ge(v_done, START + NK * b + -NK + -(-CW // P))
                    s = slice(c * CW, (c + 1) * CW)
                    nc.scalar.copy(xn_high[:, :, s], xn[:, c % XR]).then_inc(x_high, 1)

                def square_it(b, i):
                    act.wait_ge(q_high, START + NQ * b + i + 1)
                    act.wait_ge(summed, START + NQ * b + max(0, i - SR + 1))
                    nc.scalar.activation(square[:, i % SR, :], parts[:, i % PR, 0, :].bitcast(F32), ACT.Square) \
                        .then_inc(squared, 1)

                def high_parts(b):
                    split_x(b, 1)
                    for i in range(NQ):
                        n = i % PR
                        if i % 4 == 2 and i // 4 + 2 < NC:
                            split_x(b, i // 4 + 2)
                        act.wait_ge(q_done, START + NQ * b + i + 1)
                        act.wait_ge(part_stored[n], START + 16 * ((NQ // PR) * b + i // PR))
                        if i >= PR:
                            act.wait_ge(squared, START + NQ * b + i - PR + 1)
                        nc.scalar.activation(parts[:, n, 0, :], bank_q[i % 3][:, 0:CW], ACT.Copy, scale=SCALE) \
                            .then_inc(q_high, 1)
                        if i:
                            square_it(b, i - 1)
                    square_it(b, NQ - 1)

                def evacuate_v(b, more):
                    act.wait_ge(v_stored, START + VS * b)
                    for kt in range(NK):
                        if kt % 2 == 0:
                            m = keys(kt)
                            act.wait_ge(v_done, START + NK * b + kt + 1)
                            nc.scalar.copy(v_st[0:m, :, kt, :],
                                           bank_v[0][0:m, 0:C].rearrange("p (g n) -> p g n", g=G)).then_inc(v_act, 1)
                        if more and kt in CHUNK_AFTER:
                            evacuate_x(b + 1, CHUNK_AFTER[kt])
                        if more and kt == NORM0 + 1:
                            split_x(b + 1, 0)

                for c in range(NC):
                    evacuate_x(0, c)
                act.wait_ge(w_loaded, START + 16)
                nc.scalar.copy(w_high[:], w[:]).then_inc(w_split, 1)
                split_x(0, 0)
                act.wait_ge(v_zero, START + 1)
                with act.Fori(0, B - 1) as i:
                    b = Turn(act, i)
                    high_parts(b)
                    evacuate_v(b, True)
                high_parts(B - 1)
                evacuate_v(B - 1, False)

            @block.gpsimd
            def _(pool):
                def split_x(b):
                    for c in range(NC):
                        pool.wait_ge(x_high, START + NC * b + c + 1)
                        s = slice(c * CW, (c + 1) * CW)
                        nc.gpsimd.tensor_tensor(xn_low[:, :, s], xn[:, c % XR], xn_high[:, :, s].bitcast(F32), ALU.subtract) \
                            .then_inc(x_low, 1)

                nc.gpsimd.memset(v_st[KLAST:P, :, NK - 1, :], 0.0).then_inc(v_zero, 1)
                pool.wait_ge(v_zero, START + 1)
                gn.rstd(pool, 0)
                with pool.Fori(0, B - 1) as i:
                    b = Turn(pool, i)
                    split_x(b)
                    pool.wait_ge(normed, START + CH * NC * (b + 1))
                    gn.rstd(pool, b + 1)
                split_x(B - 1)
                pool.wait_ge(end_dve, START + 3 + 4)
                nc.gpsimd.partition_all_reduce(worst[:, 1:2], worst[:, 0:1], P, bass.bass_isa.ReduceOp.max) \
                    .then_inc(end_pool, 1)

            @block.vector
            def _(dve):
                v = nc.vector

                def evacuate_x(b, c):
                    if c == 0 and not isinstance(b, int):
                        dve.wait_ge(normed, START + CH * NC * b)
                        dve.wait_ge(x_stored, START + 16 * b)
                    dve.wait_ge(t_done, START + CH * (NC * b + c + 1))
                    v.tensor_copy(xT[:, 1, c * CW:(c + 1) * CW], bank_t[1][:, 0:CW]).then_inc(t_dve, 1)
                    dve.wait_ge(t_act, START + NC * b + c + 1)
                    gn.stats(xT, c, 0)
                    dve.wait_ge(t_dve, START + NC * b + c + 1)
                    gn.stats(xT, c, 1)

                def norm(b, c):
                    if c == 0:
                        dve.wait_ge(gn.rstd_done, START + 1 * (b + 1))
                        v.tensor_tensor(k["xn_mean"][:, :, at(b)], gn.off[:], gn.rstd_t[:], ALU.mult) \
                            .then_inc(mean_saved, 1)
                    dve.wait_ge(x_low, START + NC * b + max(0, c - XR + 1))
                    for ch in range(CH):
                        gn.norm(xn[:, c % XR, ch, :], xT, c, ch).then_inc(normed, 1)

                def take_max(b, i):
                    dve.wait_ge(summed, START + NQ * b + i + 1)
                    v.reduce_max(item_max[:, i:i + 1], bank_n[:, 0:CW], AX.X).then_inc(max_taken, 1)

                def low_parts(b):
                    norm(b, 1)
                    for i in range(NQ):
                        n = i % PR
                        if i % 4 == 1 and i // 4 + 2 < NC:
                            norm(b, i // 4 + 2)
                        if i >= 3:
                            take_max(b, i - 3)
                        dve.wait_ge(q_high, START + NQ * b + i + 1)
                        v.scalar_tensor_tensor(out=parts[:, n, 1, :], in0=bank_q[i % 3][:, 0:CW], scalar=SCALE,
                                               in1=parts[:, n, 0, :].bitcast(F32), op0=ALU.mult,
                                               op1=ALU.subtract).then_inc(q_low, 1)
                    for i in range(NQ - 3, NQ):
                        take_max(b, i)
                    dve.wait_ge(max_taken, START + NQ * (b + 1))
                    v.tensor_reduce(k["norm_max"][:, at(b), :], item_max[:].rearrange("p (c j) -> p j c", j=4),
                                    AX.X, ALU.max).then_inc(image_max, 1)

                def values(b, more):
                    dve.wait_ge(v_stored, START + VS * b)
                    for kt in range(1, NK, 2):
                        dve.wait_ge(v_done, START + NK * b + kt + 1)
                        v.tensor_copy(v_st[:, :, kt, :], bank_v[1][:, 0:C].rearrange("p (g n) -> p g n", g=G)) \
                            .then_inc(v_dve, 1)
                        if more and kt in CHUNK_AFTER:
                            evacuate_x(b + 1, CHUNK_AFTER[kt])
                            if CHUNK_AFTER[kt] == NC - 1:
                                gn.aggregate(dve, b + 1)
                        if more and kt == SPREAD_DVE:
                            gn.spread(dve, b + 1)
                        if more and kt == VARIANCE:
                            gn.variance(dve, b + 1)
                        if more and kt == NORM0:
                            norm(b + 1, 0)

                for c in range(NC):
                    evacuate_x(0, c)
                gn.aggregate(dve, 0)
                gn.spread(dve, 0)
                gn.variance(dve, 0)
                dve.wait_ge(w_split, START + 1)
                v.tensor_tensor(w_low[:], w[:], w_high[:].bitcast(F32), ALU.subtract).then_inc(w_split, 1)
                norm(0, 0)
                with dve.Fori(0, B - 1) as i:
                    b = Turn(dve, i)
                    low_parts(b)
                    dve.wait_ge(image_max, START + 1 * (b + 1))
                    values(b, True)
                low_parts(B - 1)
                values(B - 1, False)

                n = G * B
                dve.wait_ge(end_pe, START + 1)
                v.tensor_scalar(kmean2[:], bank_n[:, 0:n], SCALE, None, ALU.mult).then_inc(end_dve, 1)
                dve.wait_ge(end_dve, START + 1)
                v.tensor_tensor(kmean2[:], kmean2[:], kmean2[:], ALU.mult).then_inc(end_dve, 1)
                dve.wait_ge(image_max, START + B)
                q2 = k["norm_max"][:, 0:B, 0:G]
                k2 = k["norm_max"][:, 0:B, G:2 * G]
                v.scalar_tensor_tensor(out=bound[:, 0:n].rearrange("p (b g) -> p b g", g=G), in0=q2,
                                       scalar=(SLACK / SCORE_BOUND) ** 2, in1=k2, op0=ALU.mult, op1=ALU.mult) \
                    .then_inc(end_dve, 1)
                dve.wait_ge(end_pe, START + 2)
                v.scalar_tensor_tensor(out=bound[:, n:2 * n].rearrange("p (b g) -> p b g", g=G), in0=q2,
                                       scalar=(SLACK / MEAN_BOUND) ** 2,
                                       in1=bank_q[0][:, 0:n].rearrange("p (g b) -> p b g", g=G),
                                       op0=ALU.mult, op1=ALU.mult).then_inc(end_dve, 1)
                v.tensor_reduce(worst[:, 0:1], w[:, :, 2 * C:3 * C], AX.XY, ALU.max, apply_absolute_value=True) \
                    .then_inc(end_dve, 1)
                dve.wait_ge(end_dve, START + 5)
                v.tensor_scalar(bound[:, 2 * n:2 * n + 1], worst[:, 0:1], 1.0 / WV_BOUND, None, ALU.mult) \
                    .then_inc(end_dve, 1)
                dve.wait_ge(end_dve, START + 6)
                v.reduce_max(worst[:, 0:1], bound[:, 0:2 * n + 1], AX.X).then_inc(end_dve, 1)
                dve.wait_ge(end_pool, START + 1)
                v.tensor_scalar(k["bounded"][:], worst[:, 1:2], 1.0, None, ALU.is_le).then_inc(end_dve, 1)


def part_b(nc, k, B, d):
    NP = 2 * NK
    U = G * NC
    SLOTS = 3
    RING = 5
    NG = 3
    GROUP = [NK // NG * j for j in range(NG)] + [NK]
    ADDS = 2 * (NK - NG)
    AHEAD = 6
    PIECE = [0, 3, 6, 12, 18, NK]
    PIECES = len(PIECE) - 1
    with ExitStack() as ctx:
        def sb(name, shape, dt=F32):
            return ctx.enter_context(nc.sbuf_tensor("b_" + name, shape, dt))

        sems = []

        def sem(name):
            sems.append(ctx.enter_context(nc.semaphore("b_" + name)))
            return sems[-1]

        scores = ctx.enter_context(nc.psum_tensor("b_scores", [P, SLOTS, 2, 512], F32))
        out_ps = ctx.enter_context(nc.psum_tensor("b_out", [P, 512], F32))
        sum_ps = ctx.enter_context(nc.psum_tensor("b_sum", [P, 512], F32))
        k_st = [sb(f"k_st{g}", [P, HG, T], F32R) for g in range(G)]
        v_st = [sb(f"v_st{g}", [P, NK, HG * HD]) for g in range(G)]
        q_st = sb("q_st", [P, 2, HG, CW], F32R)
        prob = sb("prob", [P, RING, HG, CW])
        part = sb("part", [P, 2, HG, CW])
        res = sb("res", [P, 2, 2, CW])
        run_max = prob[:, 0]
        all_max = sb("all_max", [P, HG, CW])

        k_loaded = [[sem(f"k_loaded{g}_{n}") for n in range(PIECES)] for g in range(G)]
        v_loaded = [[sem(f"v_loaded{g}_{n}") for n in range(PIECES)] for g in range(G)]
        q_loaded = [sem(f"q_loaded{s}") for s in range(2)]
        scored, exps, pv_done, added = sem("scored"), sem("exps"), sem("pv_done"), sem("added")
        summed, sum_copied, out_copied = sem("summed"), sem("sum_copied"), sem("out_copied")
        res_stored = [sem(f"res_stored{s}") for s in range(2)]
        max_read, max_all, shifted, gate = sem("max_read"), sem("max_all"), sem("shifted"), sem("gate")

        def image_units(eng, b, unit):
            def one(g, l, i, ahead):
                u = Turn(eng, eng.snap(U * b + l + 2 * i))
                unit(g, u, l % 2, Turn(eng, eng.snap(U // 2 * b + l // 2 + i)), ahead)

            for g in range(G):
                with eng.Fori(0, NC // 2) as i:
                    for r in range(2):
                        one(g, g * NC + r, i, None)
                one(g, g * NC + NC - 1, 0, 1 - g)

        def branch(eng, fast, exact):
            ok = eng.value_load(k["bounded"][0:1, 0:1])
            with eng.If(ok > 0):
                fast()
            with eng.Else():
                exact()

        def loads(sp, pairs):
            def load_k(b, g):
                for n in range(PIECES):
                    kt0, kt1 = PIECE[n], PIECE[n + 1]
                    cols = slice(kt0 * P, min(kt1 * P, T))
                    for rep in range(2):
                        for s in range(2):
                            row = 64 * rep + 32 * s
                            sp.dma_start(k_st[g][row:row + 32, :, cols].bitcast(F32),
                                         d["k"][at(b), g, s, :, cols].rearrange("(h e) t -> e h t", e=HD)) \
                                .then_inc(k_loaded[g][n], 16)
                    sp.dma_start(v_st[g][:, kt0:kt1, :], d["v"][at(b), g, :, kt0:kt1, :]).then_inc(v_loaded[g][n], 16)

            def load_q(b, l):
                g, c = divmod(l, NC)
                for s in range(2):
                    for rep in range(2):
                        row = 64 * s + 32 * rep
                        sp.dma_start(q_st[row:row + 32, l % 2].bitcast(F32),
                                     d["q"][at(b), g, s, :, c * CW:(c + 1) * CW].rearrange("(h e) t -> e h t", e=HD)) \
                            .then_inc(q_loaded[l % 2], 16)

            def image(b, more):
                first = Turn(sp, U * b)
                sp.wait_ge(scored, START + pairs * first)
                sp.wait_ge(pv_done, START + NK * (first + 1))
                load_k(b, 1)
                for l in range(U):
                    u = first + l
                    sp.wait_ge(scored, START + pairs * u)
                    if l + 1 < U:
                        load_q(b, l + 1)
                    elif more:
                        load_q(b + 1, 0)
                    else:
                        sp.sem_inc(q_loaded[0], 64)
                    if l == NC:
                        sp.wait_ge(pv_done, START + NK * (u + 1))
                        if more:
                            load_k(b + 1, 0)
                        else:
                            sp.sem_inc(k_loaded[0][0], 64)
                    g, c = divmod(l, NC)
                    sp.wait_ge(out_copied, START + 1 * (u + 1))
                    sp.dma_start(d["att"][at(b), g, :, c * CW:(c + 1) * CW], res[:, l % 2, 0, :]) \
                        .then_inc(res_stored[l % 2], 16)
                    sp.wait_ge(sum_copied, START + 1 * (u + 1))
                    sp.dma_start(d["sums"][at(b), g, :, c * CW:(c + 1) * CW], res[0:P:HD, l % 2, 1, :]) \
                        .then_inc(res_stored[l % 2], 16)

            load_q(0, 0)
            load_k(0, 0)
            with sp.Fori(0, B - 1) as i:
                b = Turn(sp, i)
                image(b, True)
            image(B - 1, False)
            for s in range(2):
                sp.wait_ge(res_stored[s], START + 32 * (U // 2) * B)

        def score_pair(g, slot, p):
            kt, hp = divmod(p, 2)
            m = keys(kt)
            for e in range(2):
                h = 2 * hp + e
                last = nc.tensor.matmul(scores[0:m, p % SLOTS, e, 0:CW], k_st[g][:, h, kt * P:kt * P + m],
                                        q_st[:, slot, h, :], start=True, stop=True)
            last.then_inc(scored, 1)

        def weighted_values(pe, u, g, kt):
            pe.wait_ge(exps, START + NP * (u + 1) + 2 * kt + 2)
            if kt == 0:
                pe.wait_ge(out_copied, START + 1 * u)
            for h in range(HG):
                last = nc.tensor.matmul(out_ps[h * HD:(h + 1) * HD, 0:CW], v_st[g][:, kt, h * HD:(h + 1) * HD],
                                        prob[:, kt % RING, h, :], start=kt == 0, stop=kt == NK - 1)
            last.then_inc(pv_done, 1)

        def adds_until(kt, hp):
            if kt < 0:
                return adds_until(kt + NK, hp) - ADDS
            j = max(j for j in range(NG) if GROUP[j] <= kt)
            return 2 * (GROUP[j] - j + max(0, kt - GROUP[j] - 1)) + hp + 1

        def part_slot(slot, j):
            return (NG * slot + j) % 2

        def row_sums(pe, u, slot, j):
            half = part[:, part_slot(slot, j)]
            pe.wait_ge(added, START + ADDS * (u + 1) + adds_until(GROUP[j + 1] - 1, 1))
            if j == 0:
                pe.wait_ge(sum_copied, START + 1 * u)
            for h in range(HG):
                last = nc.tensor.matmul(sum_ps[h * HD:(h + 1) * HD, 0:CW], k["ones"][:], half[:, h, :],
                                        start=j == 0, stop=j == NG - 1)
            last.then_inc(summed, 1)

        def row_sums_behind(pe, u, slot, kt):
            if kt - 1 in GROUP[1:NG]:
                row_sums(pe, u, slot, GROUP.index(kt - 1) - 1)

        def add_probs(dve, u, slot, kt):
            if kt in GROUP:
                return
            j = max(j for j in range(NG) if GROUP[j] <= kt)
            rows = keys(kt)
            for hp in range(2):
                hs = slice(2 * hp, 2 * hp + 2)
                out = part[:, part_slot(slot, j), hs, :]
                dve.wait_ge(exps, START + NP * (u + 1) + 2 * kt + hp + 1)
                if kt == GROUP[j] + 1:
                    dve.wait_ge(summed, START + NG * (u + 1) + j - 1)
                    nc.vector.tensor_tensor(out, prob[:, (kt - 1) % RING, hs, :], prob[:, kt % RING, hs, :],
                                            ALU.add).then_inc(added, 1)
                else:
                    dve.wait_ge(added, START + ADDS * (u + 1) + adds_until(kt, hp) - 2)
                    nc.vector.tensor_tensor(out[0:rows], out[0:rows], prob[0:rows, kt % RING, hs, :], ALU.add) \
                        .then_inc(added, 1)

        def tile_free(eng, u, kt, hp):
            eng.wait_ge(pv_done, START + NK * (u + 1) + kt - RING + 1)
            eng.wait_ge(added, START + ADDS * (u + 1) + adds_until(kt - RING, hp))

        def copy_out(eng, copy, u, slot, use):
            eng.wait_ge(res_stored[slot], START + 32 * use)
            eng.wait_ge(pv_done, START + NK * (u + 2))
            copy(res[:, slot, 0, :], out_ps[:, 0:CW]).then_inc(out_copied, 1)

        def copy_sums(eng, copy, u, slot):
            eng.wait_ge(summed, START + NG * (u + 2))
            copy(res[:, slot, 1, :], sum_ps[:, 0:CW]).then_inc(sum_copied, 1)

        with nc.Block() as block:
            @block.sync
            def _(sp):
                for s in sems:
                    sp.sem_inc(s, START)

                branch(sp, lambda: loads(sp, NP), lambda: loads(sp, 2 * NP))

            @block.tensor
            def _(pe):
                image = []

                def fast():
                    def unit(g, u, slot, use, ahead):
                        def score(p):
                            if p == NP:
                                pe.wait_ge(q_loaded[1 - slot], START + 64 * (use + 1 + (slot == 1)))
                                if ahead is not None:
                                    k_piece(ahead, image[0] + (ahead == 0), 0)
                            if p >= NP:
                                n = p - NP
                                user = n - SLOTS if n >= SLOTS else NP - 1 - (NP - 1 - n) % SLOTS - NP
                                pe.wait_ge(exps, START + NP * (u + 2) + user + 1)
                                score_pair(g if ahead is None else ahead, 1 - slot, n)
                                return
                            if p % 2 == 0 and p // 2 in PIECE:
                                k_piece(g, image[0], PIECE.index(p // 2))
                            pe.wait_ge(exps, START + NP * (u + 1) + p - SLOTS + 1)
                            score_pair(g, slot, p)

                        for kt in range(NK):
                            values_of(g, u, slot, kt)
                            score(2 * kt + AHEAD)
                            score(2 * kt + AHEAD + 1)
                        row_sums(pe, u, slot, NG - 1)

                    def k_piece(g, b, n):
                        pe.wait_ge(k_loaded[g][n], START + 64 * (b + 1))

                    def values_of(g, u, slot, kt):
                        if kt in PIECE:
                            pe.wait_ge(v_loaded[g][PIECE.index(kt)], START + 16 * (image[0] + 1))
                        weighted_values(pe, u, g, kt)
                        row_sums_behind(pe, u, slot, kt)

                    pe.sem_inc(pv_done, NK)
                    pe.sem_inc(summed, NG)
                    pe.wait_ge(q_loaded[0], START + 64)
                    pe.wait_ge(k_loaded[0][0], START + 64)
                    for p in range(AHEAD):
                        if p >= SLOTS:
                            pe.wait_ge(exps, START + NP + p - SLOTS + 1)
                        score_pair(0, 0, p)
                    with pe.Fori(0, B) as i:
                        b = Turn(pe, i)
                        image[:] = [b]
                        image_units(pe, b, unit)

                def exact():
                    def unit(g, u, slot, use, ahead):
                        pe.wait_ge(q_loaded[slot], START + 64 * (use + 1))
                        for n in range(PIECES):
                            pe.wait_ge(k_loaded[g][n], START + 64 * (image[0] + 1))
                            pe.wait_ge(v_loaded[g][n], START + 16 * (image[0] + 1))
                        pe.wait_ge(shifted, START + NP * u)
                        for p in range(NP):
                            if p >= SLOTS:
                                pe.wait_ge(max_read, START + NP * u + p - SLOTS + 1)
                            score_pair(g, slot, p)
                        for p in range(NP):
                            if p >= SLOTS:
                                pe.wait_ge(shifted, START + NP * u + p - SLOTS + 1)
                            else:
                                pe.wait_ge(max_read, START + NP * (u + 1))
                            score_pair(g, slot, p)
                            if p % 2 and p > 2:
                                weighted_values(pe, u, g, p // 2 - 1)
                                row_sums_behind(pe, u, slot, p // 2 - 1)
                        weighted_values(pe, u, g, NK - 1)
                        row_sums(pe, u, slot, NG - 1)

                    pe.sem_inc(pv_done, NK)
                    pe.sem_inc(summed, NG)
                    with pe.Fori(0, B) as i:
                        b = Turn(pe, i)
                        image[:] = [b]
                        image_units(pe, b, unit)

                branch(pe, fast, exact)

            @block.scalar
            def _(act):
                def fast():
                    def exp(u, p):
                        kt, hp = divmod(p, 2)
                        m = keys(kt)
                        act.wait_ge(scored, START + NP * u + p + 1)
                        tile_free(act, u, kt, hp)
                        nc.scalar.activation(prob[0:m, kt % RING, 2 * hp:2 * hp + 2, :],
                                             scores[0:m, p % SLOTS, :, 0:CW], ACT.Exp, bias=-SHIFT) \
                            .then_inc(exps, 1)

                    def unit(g, u, slot, use, ahead):
                        for p in range(AHEAD, NP):
                            exp(u, p)
                        for p in range(AHEAD):
                            exp(u + 1, p)
                            if p == AHEAD - 3:
                                copy_out(act, nc.scalar.copy, u, slot, use)
                        copy_sums(act, nc.scalar.copy, u, slot)

                    act.sem_inc(exps, NP)
                    for p in range(AHEAD):
                        exp(0, p)
                    with act.Fori(0, B) as i:
                        b = Turn(act, i)
                        image_units(act, b, unit)

                def exact():
                    def unit(g, u, slot, use, ahead):
                        for p in range(NP):
                            kt, hp = divmod(p, 2)
                            m = keys(kt)
                            act.wait_ge(shifted, START + NP * u + p + 1)
                            tile = prob[0:m, kt % RING, 2 * hp:2 * hp + 2, :]
                            nc.scalar.activation(tile, tile, ACT.Exp).then_inc(exps, 1)

                    act.sem_inc(exps, NP)
                    with act.Fori(0, B) as i:
                        b = Turn(act, i)
                        image_units(act, b, unit)

                branch(act, fast, exact)

            @block.vector
            def _(dve):
                def fast():
                    def unit(g, u, slot, use, ahead):
                        for kt in range(NK):
                            add_probs(dve, u, slot, kt)

                    dve.sem_inc(added, ADDS)
                    with dve.Fori(0, B) as i:
                        b = Turn(dve, i)
                        image_units(dve, b, unit)

                def exact():
                    def unit(g, u, slot, use, ahead):
                        for p in range(NP):
                            kt, hp = divmod(p, 2)
                            m = keys(kt)
                            src = scores[0:m, p % SLOTS, :, 0:CW]
                            hs = slice(2 * hp, 2 * hp + 2)
                            dve.wait_ge(scored, START + 2 * NP * u + p + 1)
                            if kt == 0:
                                nc.vector.tensor_copy(run_max[:, hs, :], src).then_inc(max_read, 1)
                            else:
                                dve.wait_ge(max_read, START + NP * u + p - 1)
                                nc.vector.tensor_tensor(run_max[0:m, hs, :], src, run_max[0:m, hs, :], ALU.max) \
                                    .then_inc(max_read, 1)
                        dve.wait_ge(max_all, START + 1 * (u + 1))
                        for p in range(NP + 2 * 2):
                            if p < NP:
                                kt, hp = divmod(p, 2)
                                m = keys(kt)
                                hs = slice(2 * hp, 2 * hp + 2)
                                dve.wait_ge(scored, START + 2 * NP * u + NP + p + 1)
                                tile_free(dve, u, kt, hp)
                                nc.vector.tensor_tensor(prob[0:m, kt % RING, hs, :], scores[0:m, p % SLOTS, :, 0:CW],
                                                        all_max[0:m, hs, :], ALU.subtract).then_inc(shifted, 1)
                            if p >= 4 and p % 2:
                                add_probs(dve, u, slot, (p - 4) // 2)
                        copy_out(dve, nc.vector.tensor_copy, u, slot, use)
                        copy_sums(dve, nc.vector.tensor_copy, u, slot)

                    dve.sem_inc(added, ADDS)
                    with dve.Fori(0, B) as i:
                        b = Turn(dve, i)
                        image_units(dve, b, unit)

                branch(dve, fast, exact)

            @block.gpsimd
            def _(pool):
                def exact():
                    with pool.Fori(0, B * U) as i:
                        u = Turn(pool, i)
                        pool.wait_ge(max_read, START + NP * (u + 1))
                        pool.wait_ge(shifted, START + NP * u)
                        pool.sem_inc(gate, 1)
                        nc.gpsimd.partition_all_reduce(all_max[:].rearrange("p h t -> p (h t)"),
                                                       run_max.rearrange("p h t -> p (h t)"), P,
                                                       bass.bass_isa.ReduceOp.max).then_inc(max_all, 1)

                ok = pool.value_load(k["bounded"][0:1, 0:1])
                with pool.If(ok < 1):
                    exact()


def part_c(nc, k, B, d, w_proj, Wf, bf, Wg, bg, Wh, bh, out):
    with ExitStack() as ctx:
        def sb(name, shape, dt=F32):
            return ctx.enter_context(nc.sbuf_tensor("c_" + name, shape, dt))

        sems = []

        def sem(name):
            sems.append(ctx.enter_context(nc.semaphore("c_" + name)))
            return sems[-1]

        bank = [ctx.enter_context(nc.psum_tensor(f"c_bank{i}", [P, 512], F32)) for i in range(8)]
        bank_p, bank_fg, bank_s, bank_h, bank_o = bank[0:2], bank[2], bank[3], bank[4:6], bank[6:8]
        CK = Wf.shape[1]
        AR = 3
        HR = 3
        att = sb("att", [P, AR, G, CW])
        inv = sb("inv", [P, AR, G, CW])
        att_high = sb("att_high", [P, AR, G, CW], F32R)
        att_low = sb("att_low", [P, AR, G, CW], F32R)
        flat = sb("flat", [P, B, G * HG * T // P])
        yT = sb("yT", [P, CH, T])
        yn = sb("yn", [P, CH, T])
        yn_high = sb("yn_high", [P, HR, CH, CW], F32R)
        yn_low = sb("yn_low", [P, HR, CH, CW], F32R)
        y_nat = sb("y_nat", [TW, NT, C])
        fg = sb("fg", [CK, 2, 2, CW])
        sig = sb("sig", [TW, 2, TPC, TW])
        weights = sb("weights", [TW, 2, TPC, TW])
        h_sb = sb("h_sb", [TW, 2, TPC, C])
        z = sb("z", [TW, 2, TPC, C])
        FG, H_, WN = C, C + 2 * CK, 2 * C + 2 * CK
        w_all = sb("w_all", [P, CH, WN])
        w_high = sb("w_high", [P, CH, WN], F32R)
        w_low = sb("w_low", [P, CH, WN], F32R)
        bias_fg = sb("bias_fg", [2 * CK, 1])
        bias_h = sb("bias_h", [TW, 2, C])

        w_loaded = sem("w_loaded")
        x_loaded = [sem(f"x_loaded{c}") for c in range(NC)]
        att_loaded = [sem(f"att_loaded{c}") for c in range(NC)]
        sums_loaded = [sem(f"sums_loaded{b}") for b in range(B)]
        w_split = sem("w_split")
        inv_done, att_done = sem("inv_done"), sem("att_done")
        att_split_high, att_split = sem("att_split_high"), sem("att_split")
        yn_split_high, yn_split = sem("yn_split_high"), sem("yn_split")
        inv_stored = [sem(f"inv_stored{b}") for b in range(B)]
        p_done, y_done, normed = sem("p_done"), sem("y_done"), sem("normed")
        tr_done, tr_read = sem("tr_done"), sem("tr_read")
        fg_done, fg_read, s_done, sig_done, masked = (sem("fg_done"), sem("fg_read"), sem("s_done"),
                                                      sem("sig_done"), sem("masked"))
        h_done, h_read, o_done, z_done = sem("h_done"), sem("h_read"), sem("o_done"), sem("z_done")
        z_stored = [sem(f"z_stored{s}") for s in range(2)]
        gn = GroupNorm(nc, sb, sem, k, bank_p[0])
        NP2 = NT // 2
        MEANS, SPREAD = 4, 7
        out_tok = out.rearrange("b h w c -> b (h w) c").rearrange("b (t p) c -> b p t c", p=TW)

        def before(c, slots):
            return max(0, c - slots + 1)

        def slot_users(c):
            return max(0, c - 1)

        with nc.Block() as block:
            @block.sync
            def _(sp):
                for s in sems:
                    sp.sem_inc(s, START)

                def load(b, c):
                    s = slice(c * CW, (c + 1) * CW)
                    sp.wait_ge(att_split, START + NC * b + before(c, AR))
                    sp.dma_start(att[:, c % AR], d["att"][at(b), :, :, s].rearrange("g p t -> p g t")) \
                        .then_inc(att_loaded[c], 16)
                    for h in range(HG):
                        src = d["inv"][at(b), :, h:h + 1, s].rearrange("g a t -> a g t")
                        sp.dma_start(inv[h * HD:(h + 1) * HD, c % AR], src.broadcast_to([HD, G, CW])) \
                            .then_inc(att_loaded[c], 16)
                    if not (isinstance(b, int) and b == 0):
                        sp.wait_ge(normed, START + NP2 * b)
                        sp.wait_ge(tr_done, START + NP2 * b)
                    sp.dma_start(yT[:, :, s], d["xT"][at(b), :, :, s].rearrange("h p t -> p h t")) \
                        .then_inc(x_loaded[c], 16)

                def store(b, c):
                    sp.wait_ge(z_done, START + NP2 * b + 2 * (c + 1))
                    sp.dma_start(out_tok[at(b), :, c * TPC:(c + 1) * TPC, :], z[:, c % 2]).then_inc(z_stored[c % 2], 16)

                def image(b, more):
                    for c in range(NC + 2):
                        if more and c < NC:
                            load(b + 1, c)
                        if c >= 2:
                            store(b, c - 2)

                sp.dma_start(w_all[:, :, 0:C], w_proj.rearrange("(h p) n -> p h n", p=P)).then_inc(w_loaded, 16)
                sp.dma_start(w_all[:, :, FG:FG + CK], Wf.rearrange("(h p) n -> p h n", p=P)).then_inc(w_loaded, 16)
                sp.dma_start(w_all[:, :, FG + CK:H_], Wg.rearrange("(h p) n -> p h n", p=P)).then_inc(w_loaded, 16)
                sp.dma_start(w_all[:, :, H_:], Wh.rearrange("(h p) n -> p h n", p=P)).then_inc(w_loaded, 16)
                sp.dma_start(bias_fg[0:CK], bf.rearrange("(p a) -> p a", a=1)).then_inc(w_loaded, 16)
                sp.dma_start(bias_fg[CK:], bg.rearrange("(p a) -> p a", a=1)).then_inc(w_loaded, 16)
                for e in range(2):
                    sp.dma_start(bias_h[:, e, :], bh.rearrange("(a n) -> a n", a=1).broadcast_to([TW, C])) \
                        .then_inc(w_loaded, 16)
                spread = lambda t: t.rearrange("g h t -> (g h t)").rearrange("(p n) -> p n", p=P)
                for b in range(B):
                    sp.dma_start(flat[:, b, :], spread(d["sums"][b])).then_inc(sums_loaded[b], 16)
                for b in range(B):
                    sp.wait_ge(inv_done, START + b + 1)
                    sp.dma_start(spread(d["inv"][b]), flat[:, b, :]).then_inc(inv_stored[b], 16)
                for b in range(B):
                    sp.wait_ge(inv_stored[b], START + 16)
                for c in range(NC):
                    load(0, c)
                with sp.Fori(0, B - 1) as i:
                    b = Turn(sp, i)
                    image(b, True)
                image(B - 1, False)
                sp.wait_ge(z_stored[0], START + 16 * ((NC + 1) // 2) * B)
                sp.wait_ge(z_stored[1], START + 16 * (NC // 2) * B)

            @block.tensor
            def _(pe):
                def project(b, c):
                    pe.wait_ge(att_split, START + NC * b + c + 1)
                    for ch in range(CH):
                        pe.wait_ge(y_done, START + NP2 * b + max(0, 2 * c + ch - 1))
                        ws = slice(ch * P, (ch + 1) * P)
                        for g in range(G):
                            last = three_passes(nc, bank_p[ch][:, 0:CW], (w_high[:, g, ws], w_low[:, g, ws]),
                                                (att_high[:, c % AR, g, :], att_low[:, c % AR, g, :]),
                                                g == 0, g == G - 1)
                        last.then_inc(p_done, 1)

                def transposes(b):
                    for i in range(NP2):
                        pe.wait_ge(y_done, START + NP2 * b + 2 * (i // 2 + 1))
                        if i < 2:
                            pe.wait_ge(z_done, START + NP2 * b)
                        else:
                            pe.wait_ge(tr_read, START + NP2 * b + i - 1)
                        for e in range(2):
                            for ch in range(CH):
                                t = 2 * i + e
                                last = nc.tensor.transpose(bank_o[i % 2][0:TW, e * C + ch * P:e * C + (ch + 1) * P],
                                                           yT[:, ch, t * TW:(t + 1) * TW], k["ident"][:])
                        last.then_inc(tr_done, 1)
                        if i == MEANS:
                            pe.wait_ge(y_done, START + NP2 * (b + 1))
                            gn.average_means(pe, b)
                        if i == SPREAD:
                            gn.average_spread(pe, b)

                def f_g_h_scores(b, c):
                    pe.wait_ge(yn_split, START + NC * b + c + 1)
                    pe.wait_ge(fg_read, START + 2 * (NC * b + c))
                    for ch in range(CH):
                        last = three_passes(nc, bank_fg[0:2 * CK, 0:CW], (w_high[:, ch, FG:H_], w_low[:, ch, FG:H_]),
                                            (yn_high[:, c % HR, ch, :], yn_low[:, c % HR, ch, :]),
                                            ch == 0, ch == CH - 1)
                    last.then_inc(fg_done, 1)
                    for e in range(2):
                        pe.wait_ge(h_read, START + NP2 * b + max(0, 2 * c + e - 1))
                        for t in range(2):
                            ts = slice((2 * e + t) * TW, (2 * e + t + 1) * TW)
                            for ch in range(CH):
                                last = three_passes(nc, bank_h[e][0:TW, t * C:(t + 1) * C],
                                                    (yn_high[:, c % HR, ch, ts], yn_low[:, c % HR, ch, ts]),
                                                    (w_high[:, ch, H_:], w_low[:, ch, H_:]), ch == 0, ch == CH - 1)
                        last.then_inc(h_done, 1)
                    pe.wait_ge(fg_read, START + 2 * (NC * b + c + 1))
                    pe.wait_ge(sig_done, START + NC * b + c)
                    for t in range(TPC):
                        ts = slice(t * TW, (t + 1) * TW)
                        last = nc.tensor.matmul(bank_s[0:TW, ts], fg[:, c % 2, 1, ts], fg[:, c % 2, 0, ts],
                                                start=True, stop=True)
                    last.then_inc(s_done, 1)

                def weighted_h(b, c):
                    pe.wait_ge(masked, START + NC * b + c + 1)
                    pe.wait_ge(h_read, START + NP2 * b + 2 * (c + 1))
                    for e in range(2):
                        i = 2 * c + e
                        if i < 2:
                            pe.wait_ge(tr_read, START + NP2 * (b + 1))
                        else:
                            pe.wait_ge(z_done, START + NP2 * b + i - 1)
                        for t in range(2):
                            last = nc.tensor.matmul(bank_o[e][0:TW, t * C:(t + 1) * C],
                                                    weights[:, c % 2, 2 * e + t, :], h_sb[:, c % 2, 2 * e + t, :],
                                                    start=True, stop=True)
                        last.then_inc(o_done, 1)

                def image(b, more):
                    transposes(b)
                    for c in range(NC):
                        f_g_h_scores(b, c)
                        if c:
                            weighted_h(b, c - 1)
                            if more:
                                project(b + 1, c - 1)
                    weighted_h(b, NC - 1)
                    if more:
                        project(b + 1, NC - 1)

                pe.wait_ge(w_split, START + 2)
                for c in range(NC):
                    project(0, c)
                with pe.Fori(0, B - 1) as i:
                    b = Turn(pe, i)
                    image(b, True)
                image(B - 1, False)

            @block.scalar
            def _(act):
                def split_att(b, c):
                    act.wait_ge(att_done, START + G * (NC * b + c + 1))
                    act.wait_ge(p_done, START + NP2 * b + 2 * before(c, AR))
                    nc.scalar.copy(att_high[:, c % AR], att[:, c % AR]).then_inc(att_split_high, 1)

                def split_yn(b, c):
                    act.wait_ge(normed, START + CH * (NC * b + c + 1))
                    act.wait_ge(h_done, START + NP2 * b + 2 * before(c, HR))
                    nc.scalar.copy(yn_high[:, c % HR], yn[:, :, c * CW:(c + 1) * CW]).then_inc(yn_split_high, 1)

                def image(b, more):
                    act.wait_ge(z_done, START + NP2 * b)
                    for i in range(NP2):
                        act.wait_ge(tr_done, START + NP2 * b + i + 1)
                        nc.scalar.copy(y_nat[:, 2 * i:2 * i + 2, :],
                                       bank_o[i % 2][0:TW, :].rearrange("p (t c) -> p t c", c=C)).then_inc(tr_read, 1)
                        if i in (NP2 - 3, NP2 - 1):
                            split_yn(b, int(i == NP2 - 1))
                    for c in range(NC):
                        act.wait_ge(fg_done, START + NC * b + c + 1)
                        act.wait_ge(s_done, START + NC * b + slot_users(c))
                        for n in range(2):
                            nc.scalar.activation(fg[:, c % 2, n, :], bank_fg[n * CK:(n + 1) * CK, 0:CW], ACT.Identity,
                                                 bias=bias_fg[n * CK:(n + 1) * CK, :]).then_inc(fg_read, 1)
                        if c + 2 < NC:
                            split_yn(b, c + 2)
                        act.wait_ge(s_done, START + NC * b + c + 1)
                        act.wait_ge(masked, START + NC * b + slot_users(c))
                        nc.scalar.activation(sig[:, c % 2].rearrange("p t n -> p (t n)"), bank_s[0:TW, 0:CW],
                                             ACT.Sigmoid).then_inc(sig_done, 1)
                        if more:
                            split_att(b + 1, c)

                act.wait_ge(w_loaded, START + 16 * 8)
                nc.scalar.copy(w_high[:], w_all[:]).then_inc(w_split, 1)
                for c in range(NC):
                    split_att(0, c)
                with act.Fori(0, B - 1) as i:
                    b = Turn(act, i)
                    image(b, True)
                image(B - 1, False)

            @block.gpsimd
            def _(pool):
                def image(b, more):
                    gn.rstd(pool, b)
                    for c in range(NC):
                        if more:
                            divide(b + 1, c)
                        pool.wait_ge(sig_done, START + NC * b + c + 1)
                        pool.wait_ge(o_done, START + NP2 * b + 2 * slot_users(c))
                        nc.gpsimd.tensor_tensor(weights[:, c % 2], sig[:, c % 2],
                                                k["row_mask"][0:TW, None, :].broadcast_to([TW, TPC, TW]),
                                                ALU.mult).then_inc(masked, 1)

                def divide(b, c):
                    pool.wait_ge(att_loaded[c], START + 80 * (b + 1))
                    for g in range(G):
                        s = att[:, c % AR, g, :]
                        nc.gpsimd.tensor_tensor(s, s, inv[:, c % AR, g, :], ALU.mult).then_inc(att_done, 1)

                for c in range(NC):
                    divide(0, c)
                with pool.Fori(0, B - 1) as i:
                    b = Turn(pool, i)
                    image(b, True)
                image(B - 1, False)

            @block.vector
            def _(dve):
                v = nc.vector

                def split_att(b, c):
                    dve.wait_ge(att_split_high, START + NC * b + c + 1)
                    v.tensor_tensor(att_low[:, c % AR], att[:, c % AR], att_high[:, c % AR].bitcast(F32), ALU.subtract) \
                        .then_inc(att_split, 1)

                def split_yn(b, c):
                    dve.wait_ge(yn_split_high, START + NC * b + c + 1)
                    v.tensor_tensor(yn_low[:, c % HR], yn[:, :, c * CW:(c + 1) * CW],
                                    yn_high[:, c % HR].bitcast(F32), ALU.subtract).then_inc(yn_split, 1)

                def add_residual(b, c):
                    dve.wait_ge(x_loaded[c], START + 16 * (b + 1))
                    for ch in range(CH):
                        s = yT[:, ch, c * CW:(c + 1) * CW]
                        dve.wait_ge(p_done, START + NP2 * b + 2 * c + ch + 1)
                        v.tensor_tensor(s, bank_p[ch][:, 0:CW], s, ALU.add).then_inc(y_done, 1)
                    for ch in range(CH):
                        dve.wait_ge(y_done, START + NP2 * b + 2 * c + ch + 1)
                        gn.stats(yT, c, ch)

                def norm(b):
                    gn.aggregate(dve, b)
                    gn.spread(dve, b)
                    gn.variance(dve, b)
                    dve.wait_ge(gn.rstd_done, START + 1 * (b + 1))
                    dve.wait_ge(yn_split, START + NC * b)
                    for c in range(NC):
                        for ch in range(CH):
                            gn.norm(yn[:, ch, c * CW:(c + 1) * CW], yT, c, ch).then_inc(normed, 1)

                def h_rows(b, c):
                    dve.wait_ge(o_done, START + NP2 * b + 2 * slot_users(c))
                    for e in range(2):
                        dve.wait_ge(h_done, START + NP2 * b + 2 * c + e + 1)
                        v.tensor_tensor(h_sb[:, c % 2, 2 * e:2 * e + 2, :],
                                        bank_h[e][0:TW, :].rearrange("p (t c) -> p t c", c=C), bias_h[:], ALU.add) \
                            .then_inc(h_read, 1)

                def results(b, c):
                    users = (NC + 1) // 2 if c % 2 == 0 else NC // 2
                    dve.wait_ge(z_stored[c % 2], START + 16 * (users * b + c // 2))
                    for e in range(2):
                        t = TPC * c + 2 * e
                        dve.wait_ge(o_done, START + NP2 * b + 2 * c + e + 1)
                        v.tensor_tensor(z[:, c % 2, 2 * e:2 * e + 2, :],
                                        bank_o[e][0:TW, :].rearrange("p (t c) -> p t c", c=C),
                                        y_nat[:, t:t + 2, :], ALU.add).then_inc(z_done, 1)

                def image(b, more):
                    norm(b)
                    split_yn(b, 0)
                    split_yn(b, 1)
                    dve.wait_ge(tr_read, START + NP2 * (b + 1))
                    for c in range(NC):
                        h_rows(b, c)
                        if c:
                            results(b, c - 1)
                        if c + 2 < NC:
                            split_yn(b, c + 2)
                        if more:
                            if c:
                                add_residual(b + 1, c - 1)
                            split_att(b + 1, c)
                    results(b, NC - 1)
                    if more:
                        add_residual(b + 1, NC - 1)

                for b in range(B):
                    dve.wait_ge(sums_loaded[b], START + 16)
                    v.reciprocal(flat[:, b, :], flat[:, b, :]).then_inc(inv_done, 1)
                dve.wait_ge(w_split, START + 1)
                v.tensor_tensor(w_low[:], w_all[:], w_high[:].bitcast(F32), ALU.subtract).then_inc(w_split, 1)
                for c in range(NC):
                    split_att(0, c)
                    if c:
                        add_residual(0, c - 1)
                add_residual(0, NC - 1)
                with dve.Fori(0, B - 1) as i:
                    b = Turn(dve, i)
                    image(b, True)
                image(B - 1, False)


def build(nc, x, w_qkv, w_proj, Wf, bf, Wg, bg, Wh, bh, out):
    B = x.shape[0]
    nc.disable_value_cache = True
    d = dict(
        xT=nc.dram_tensor("xT_scratch", (B, CH, P, T), F32).ap(),
        q=nc.dram_tensor("q_scratch", (B, G, 2, P, T), F32).ap(),
        k=nc.dram_tensor("k_scratch", (B, G, 2, P, T), F32).ap(),
        v=nc.dram_tensor("v_scratch", (B, G, P, NK, P), F32).ap(),
        att=nc.dram_tensor("att_scratch", (B, G, P, T), F32).ap(),
        sums=nc.dram_tensor("sums_scratch", (B, G, HG, T), F32).ap(),
        inv=nc.dram_tensor("inv_scratch", (B, G, HG, T), F32).ap(),
    )
    with ExitStack() as ctx:
        k = build_consts(nc, ctx)
        part_a(nc, k, B, x, w_qkv, d)
        part_b(nc, k, B, d)
        part_c(nc, k, B, d, w_proj, Wf, bf, Wg, bg, Wh, bh, out)


_INS = ["x", "L0_conv_w_qkv", "L0_conv_w_proj", "L1_conv_Wf", "L1_conv_bf", "L1_conv_Wg", "L1_conv_bg",
        "L1_conv_Wh", "L1_conv_bh"]


def kernel(**inputs):
    import numpy as _np
    import concourse.bacc as _bacc
    from concourse import mybir as _mybir
    from concourse.bass_utils import run_bass_kernel_spmd as _run

    nc = _bacc.Bacc("TRN2", target_bir_lowering=False, num_devices=1)
    arrays, args = {}, []
    for name in _INS:
        a = _np.ascontiguousarray(inputs[name])
        arrays[f"in_{name}"] = a
        args.append(nc.dram_tensor(f"in_{name}", a.shape, _mybir.dt.from_np(a.dtype), kind="ExternalInput").ap())
    out = nc.dram_tensor("out_y", inputs["x"].shape, _mybir.dt.float32, kind="ExternalOutput").ap()
    build(nc, *args, out)
    return _run(nc, [arrays], core_ids=[0]).results[0]["out_y"]
```
